# Optimizing a Trainium2 kernel written in Bass

```python
import numpy as np
import jax
import jax.numpy as jnp

def _softmax(x, axis=-1):
    return jax.nn.softmax(x, axis=axis)

def _gelu(x):
    return jax.nn.gelu(x, approximate=True)

def _silu(x):
    return jax.nn.silu(x)

def _sigmoid(x):
    return jax.nn.sigmoid(x)

def _layernorm(x, axis=-1, eps=1e-05):
    m = jnp.mean(x, axis=axis, keepdims=True)
    v = jnp.var(x, axis=axis, keepdims=True)
    return (x - m) / jnp.sqrt(v + eps)

def _scatter_add(tgt, idx, src, axis=0):
    return tgt.at[idx].add(src)

def _segment_sum(src, seg, n):
    return jax.ops.segment_sum(src, seg, n)
kernel_name = 'mk_gnn_preln_d1_gnn_r8_b7c4c7'

def setup_inputs(seed: int=0):
    np.random.seed(seed)
    _w = jnp.asarray

    def _rec_inputs():
        import jax
        import jax.numpy as jnp
        _gk = jax.random.key(seed)
        x = -0.0001126 + 1 * jax.random.normal(jax.random.fold_in(_gk, 1), (1250, 768), jnp.float32)
        src = jax.random.randint(jax.random.fold_in(_gk, 2), (40000,), 0, 1250, jnp.int32)
        dst = jax.random.randint(jax.random.fold_in(_gk, 3), (40000,), 0, 1250, jnp.int32)
        _o = jnp.argsort(dst, stable=True)
        src = src[_o]
        dst = dst[_o]
        edge_type_3 = jax.random.randint(jax.random.fold_in(_gk, 12), (40000,), 0, 3, jnp.int32)
        node_type_3 = jax.random.randint(jax.random.fold_in(_gk, 13), (1250,), 0, 3, jnp.int32)
        return (x, src, dst, edge_type_3, node_type_3)
    x, src, dst, edge_type_3, node_type_3 = _rec_inputs()

    def _L0_gnn_setup():
        import jax, jax.numpy as jnp
        import numpy as np
        NUM_NODES = 1250
        NUM_EDGES = 20000
        IN_CH = 768
        TYPE_DIM = 128
        HID = 768
        OUT = 768
        NUM_REL = 3
        NUM_NODE_TYPE = 3

        def _glorot(key, shape):
            fan_in, fan_out = (shape[-2], shape[-1])
            lim = (6.0 / (fan_in + fan_out)) ** 0.5
            return jax.random.uniform(key, shape, jnp.float32, -lim, lim)

        def rgcn_conv(h, src, dst, edge_type, w_rel, w_root, bias):
            num_nodes = h.shape[0]
            xw = jnp.einsum('nd,rde->rne', h, w_rel)
            msg = xw[edge_type, src]
            onehot = jax.nn.one_hot(edge_type, NUM_REL, dtype=h.dtype)
            count = jax.ops.segment_sum(onehot, dst, num_segments=num_nodes)
            inv = jnp.where(count > 0, 1.0 / jnp.maximum(count, 1.0), 0.0)
            msg = msg * inv[dst, edge_type][:, None]
            agg = jax.ops.segment_sum(msg, dst, num_segments=num_nodes)
            return agg + h @ w_root + bias
        key = jax.random.key(seed)
        ks = jax.random.split(key, 16)
        d1 = IN_CH + TYPE_DIM
        inp = {'x': jax.random.normal(ks[0], (NUM_NODES, IN_CH), jnp.float32), 'node_type': jax.random.randint(ks[1], (NUM_NODES,), 0, NUM_NODE_TYPE, jnp.int32), 'edge_index': jax.random.randint(ks[2], (2, NUM_EDGES), 0, NUM_NODES, jnp.int32), 'edge_type': jax.random.randint(ks[3], (NUM_EDGES,), 0, NUM_REL, jnp.int32), 'node_emb': jax.random.normal(ks[4], (NUM_NODE_TYPE, TYPE_DIM), jnp.float32), 'w_rel1': _glorot(ks[5], (NUM_REL, d1, d1)), 'w_root1': _glorot(ks[6], (d1, d1)), 'b1': jnp.zeros((d1,), jnp.float32), 'w_rel2': _glorot(ks[7], (NUM_REL, d1, HID)), 'w_root2': _glorot(ks[8], (d1, HID)), 'b2': jnp.zeros((HID,), jnp.float32), 'w_rel3': _glorot(ks[9], (NUM_REL, HID, OUT)), 'w_root3': _glorot(ks[10], (HID, OUT)), 'b3': jnp.zeros((OUT,), jnp.float32)}
        return inp
    _L0_gnn_all = _L0_gnn_setup()
    _L0_gnn_in = {k: v for k, v in _L0_gnn_all.items() if k in ('node_emb', 'w_rel1', 'w_root1', 'b1', 'w_rel2', 'w_root2', 'b2', 'w_rel3', 'w_root3', 'b3')}
    del _L0_gnn_all
    return {'x': x, 'src': src, 'dst': dst, 'edge_type_3': edge_type_3, 'node_type_3': node_type_3, 'L0_gnn_node_emb': _L0_gnn_in['node_emb'], 'L0_gnn_w_rel1': _L0_gnn_in['w_rel1'], 'L0_gnn_w_root1': _L0_gnn_in['w_root1'], 'L0_gnn_b1': _L0_gnn_in['b1'], 'L0_gnn_w_rel2': _L0_gnn_in['w_rel2'], 'L0_gnn_w_root2': _L0_gnn_in['w_root2'], 'L0_gnn_b2': _L0_gnn_in['b2'], 'L0_gnn_w_rel3': _L0_gnn_in['w_rel3'], 'L0_gnn_w_root3': _L0_gnn_in['w_root3'], 'L0_gnn_b3': _L0_gnn_in['b3']}

def reference(x, src, dst, edge_type_3, node_type_3, L0_gnn_node_emb, L0_gnn_w_rel1, L0_gnn_w_root1, L0_gnn_b1, L0_gnn_w_rel2, L0_gnn_w_root2, L0_gnn_b2, L0_gnn_w_rel3, L0_gnn_w_root3, L0_gnn_b3):
    import jax
    import jax.numpy as jnp

    def _L0_gnn_ref(x, node_type, edge_index, edge_type, node_emb, w_rel1, w_root1, b1, w_rel2, w_root2, b2, w_rel3, w_root3, b3):
        import jax, jax.numpy as jnp
        import numpy as np
        NUM_NODES = 1250
        NUM_EDGES = 20000
        IN_CH = 768
        TYPE_DIM = 128
        HID = 768
        OUT = 768
        NUM_REL = 3
        NUM_NODE_TYPE = 3

        def _glorot(key, shape):
            fan_in, fan_out = (shape[-2], shape[-1])
            lim = (6.0 / (fan_in + fan_out)) ** 0.5
            return jax.random.uniform(key, shape, jnp.float32, -lim, lim)

        def rgcn_conv(h, src, dst, edge_type, w_rel, w_root, bias):
            num_nodes = h.shape[0]
            xw = jnp.einsum('nd,rde->rne', h, w_rel)
            msg = xw[edge_type, src]
            onehot = jax.nn.one_hot(edge_type, NUM_REL, dtype=h.dtype)
            count = jax.ops.segment_sum(onehot, dst, num_segments=num_nodes)
            inv = jnp.where(count > 0, 1.0 / jnp.maximum(count, 1.0), 0.0)
            msg = msg * inv[dst, edge_type][:, None]
            agg = jax.ops.segment_sum(msg, dst, num_segments=num_nodes)
            return agg + h @ w_root + bias
        src, dst = (edge_index[0], edge_index[1])
        h = jnp.concatenate([x, node_emb[node_type]], axis=-1)
        h = jax.nn.relu(rgcn_conv(h, src, dst, edge_type, w_rel1, w_root1, b1))
        h = jax.nn.relu(rgcn_conv(h, src, dst, edge_type, w_rel2, w_root2, b2))
        h = jax.nn.relu(rgcn_conv(h, src, dst, edge_type, w_rel3, w_root3, b3))
        return h
    edge_index = jnp.stack([src, dst])
    h = jnp.maximum(_layernorm(x, axis=-1), 0.0)
    x = x + _L0_gnn_ref(h, node_type_3, edge_index, edge_type_3, L0_gnn_node_emb, L0_gnn_w_rel1, L0_gnn_w_root1, L0_gnn_b1, L0_gnn_w_rel2, L0_gnn_w_root2, L0_gnn_b2, L0_gnn_w_rel3, L0_gnn_w_root3, L0_gnn_b3)
    return x

_drawn_inputs = setup_inputs


def setup_inputs(seed=0):
    import zlib

    import numpy as np

    out = dict(_drawn_inputs(seed))
    spreads = {'L0_gnn_b1': (0.0, 0.1), 'L0_gnn_b2': (0.0, 0.1), 'L0_gnn_b3': (0.0, 0.1)}
    factors = {}
    for name, (base, spread) in spreads.items():
        noise = np.random.default_rng([zlib.crc32(name.encode()), seed]).standard_normal(out[name].shape)
        drawn = base * np.exp(spread * noise) if base else spread * noise
        out[name] = jnp.asarray(drawn.astype(out[name].dtype))
    for name, factor in factors.items():
        out[name] = (out[name] * factor).astype(out[name].dtype)
    return out
```

```python
from contextlib import ExitStack

import concourse.bass as bass
from concourse import mybir


P = 128
N = 1250
NODE_TILES = (N + P - 1) // P
FULL_ROWS = (NODE_TILES - 1) * P
LAST_ROWS = N - FULL_ROWS
IN_CH = 768
TYPE_DIM = 128
RELS = 3
MATS = RELS + 1
EDGES = 40000
K_TILES = (7, 7, 6)
T = (7, 6, 6)
LAYERS = 3
FIRST = (0, T[0], T[0] + T[1])
BLOCKS = sum(T)

CHUNKS = ((0, 417), (417, 417), (834, 416))
CHUNK = 417
BANK = 512
H0_CHUNKS = tuple((c, min(BANK, N - c)) for c in range(0, N, BANK))

SUB = 125
SUBS = 2
GROUPS = EDGES // (SUB * SUBS)
HALVES = 2
GP = GROUPS // HALVES
HE = EDGES // GP
WIN = 12
WIN_COLS = NODE_TILES * RELS * WIN
N_PAD = 1264
LAST_WIN = N_PAD - WIN
RING = 4
FAR_STEPS = 7
SCANS0 = 2 * K_TILES[0]
SCAN_EVERY = (GROUPS - RING) // (SCANS0 - 1)

TINY = 1e-30
EXPONENT = 0x7F800000
INVERSE_BITS = float(254 << 23)
TOP = 2.0 ** 14
K_BOUND = 1024.0
LN_BOUND = 27.8
EPS = 1e-5

F32 = mybir.dt.float32
F16 = mybir.dt.float16
I32 = mybir.dt.int32
ALU = mybir.AluOpType
ACT = mybir.ActivationFunctionType
AX = mybir.AxisListType
RMAX = bass.bass_isa.ReduceOp.max

RING_CREDIT = RING
BANK_CREDIT = 2
SLOT_CREDIT = 4
STORE_CREDIT = 64
RESID_CREDIT = 32
DONE_CREDIT = 1
SRC_CREDIT = 1

SCAN_INC = 2 * 16
OWN_INC = MATS * 16
OWN0 = SCANS0 + 2
IN0 = SCANS0 * SCAN_INC + 2 * OWN_INC
LAST = LAYERS - 1


def used_before(l, t):
    return OWN0 + 4 * (FIRST[l] + t) if l < LAST else OWN0 + 4 * FIRST[l] + 2 * t


def in_before(l, t):
    block = 2 * (SCAN_INC + OWN_INC)
    return IN0 + block * (FIRST[l] + t) if l < LAST else IN0 + block * FIRST[l] + 2 * OWN_INC * t


def scans(l):
    return 2 if l < LAST else 0


def w_scaled_at(l):
    return 2 + 2 * l


def m_scaled_at(l):
    return 3 + 2 * l


class Steps:

    def __init__(self, eng, semaphore):
        self.eng, self.semaphore, self.base, self.count = eng, semaphore, 0, 0

    def then(self, instruction):
        self.count += 1
        instruction.then_inc(self.semaphore, 1)
        self.eng.wait_ge(self.semaphore, self.base + self.count)


def gnn_kernel(nc, x, src, dst, edge_type, node_type, node_emb,
               w_rel1, w_root1, b1, w_rel2, w_root2, b2, w_rel3, w_root3, b3, out):
    bias = (b1, b2, b3)
    mats = tuple([wr[0], wr[1], wr[2], wo] for wr, wo in
                 ((w_rel1, w_root1), (w_rel2, w_root2), (w_rel3, w_root3)))

    with ExitStack() as ctx:
        def sb(name, shape, dt):
            return ctx.enter_context(nc.sbuf_tensor(name, shape, dt))

        def sem(name):
            return ctx.enter_context(nc.semaphore(name))

        counts = sb("counts", [P, NODE_TILES, RELS, N_PAD], F16)
        h_a = sb("h_a", [P, 2, 7, N], F16)
        h_b = sb("h_b", [P, 2, 7, N], F16)
        h_in = (h_a, h_b, h_a)
        msg = sb("msg", [P, NODE_TILES, 2, RELS * P], F16)
        w_split = sb("w_split", [P, 7, 2, MATS, P], F16)
        w_raw = sb("w_raw", [P, 4 * MATS * P], F32)
        inv = sb("inv", [P, RELS, N], F32)
        acc = sb("acc", [P, N], F32)
        part = sb("part", [P, CHUNK], F32)
        ident = sb("ident", [P, P], F32)
        bias_sb = sb("bias_sb", [P, BLOCKS], F32)
        W_MAX, W_SCALE, W_BACK, H_TOP, H_SCALE, H_BACK, M_SCALE, M_BACK, ROOT_BACK, REL_BACK, B1, B2 = range(12)
        sc = sb("sc", [P, LAYERS, 12], F32)
        tile_max = sb("tile_max", [P, 2 * SCANS0], F32)
        local = sb("local", [P, 2], F32)
        over_all = sb("over_all", [P, 2], F32)
        bias_max = sb("bias_max", [P, 1], F32)

        flat_a = h_a[:].rearrange("p a k n -> p (a k n)").bitcast(F32)
        flat_b = h_b[:].rearrange("p a k n -> p (a k n)").bitcast(F32)
        flat_w = w_split[:].rearrange("p k a m e -> p (k a m e)").bitcast(F32)
        flat_m = msg[:].rearrange("p j a e -> p (j a e)")
        flat_mf = flat_m.bitcast(F32)
        flat_i = inv[:].rearrange("p r n -> p (r n)")
        x_sb = flat_b[:, 0:NODE_TILES * IN_CH].rearrange("p (j c) -> p j c", j=NODE_TILES)

        def rows_of(k, n=1):
            return flat_a[0:GP, k * HE:(k + n) * HE]

        ed = rows_of(0, 3).bitcast(I32).rearrange("p (a h i) -> p a h i", a=3, h=HALVES)
        src_hi = rows_of(3).bitcast(I32)
        src_lo = rows_of(4).bitcast(I32)
        keys = rows_of(5, 4).rearrange("p (a h u i) -> p a h u i", a=4, h=HALVES, u=SUBS)
        key_tmp = rows_of(9)
        lowest = flat_a[0:GP, 10 * HE:10 * HE + HALVES]
        highest = flat_a[0:GP, 10 * HE + 2:10 * HE + 2 + HALVES]
        extra = flat_a[0:GP, 10 * HE + 4:10 * HE + 4 + HALVES]
        keys_t = flat_w[0:SUB, 0:4 * SUBS * GROUPS].rearrange("p (a u g) -> p a u g", a=4, u=SUBS)
        ones_h = flat_w[:, 4 * SUBS * GROUPS:4 * SUBS * GROUPS + P // 2].bitcast(F16)
        ring_main = flat_m[:, 0:RING * SUBS * WIN_COLS].rearrange("p (s u c) -> p s u c", s=RING, u=SUBS)
        ring_src = flat_m[:, RING * SUBS * WIN_COLS:RING * SUBS * (WIN_COLS + P)].rearrange(
            "p (s u c) -> p s u c", s=RING, u=SUBS)
        stats = flat_mf[:, 2000:2120].rearrange("p (j s) -> p j s", j=NODE_TILES)
        mean_var = flat_mf[:, 2120:2140].rearrange("p (j s) -> p j s", j=NODE_TILES)
        var_eps, std, rstd, newton, newton2 = (flat_mf[:, 2140 + 10 * k:2150 + 10 * k] for k in range(5))
        bias_rows = flat_mf[0:BLOCKS, 2200:2200 + P]
        hot_type = flat_mf[0:RELS, 2500:2500 + N]
        iota_i = flat_i[:, 0:WIN_COLS].bitcast(I32)
        iota_h = flat_i[:, 400:400 + WIN_COLS // 2].bitcast(F16)
        row_f = flat_i[0:1, 600:600 + 2 * GROUPS].rearrange("p (a g) -> p a g", a=2)
        row_i = flat_i[0:1, 1000:1000 + GROUPS].bitcast(I32)
        most_f = flat_i[0:1, 1200:1201]
        most_i = flat_i[0:1, 1204:1205].bitcast(I32)
        far = flat_i[0:SUB, 1300:1308]
        ring_keys = flat_i[0:SUB, 1320:1320 + SUBS * RING].rearrange("p (u s) -> p u s", u=SUBS)
        gate = flat_i[0:SUB, 1340:1341 + RING]
        part_id_i = flat_i[:, 1310:1311].bitcast(I32)
        part_id = flat_i[:, 1312:1313]
        type_i = acc[0:RELS, :].bitcast(I32)
        emb = part[0:RELS, 0:TYPE_DIM]
        resid = flat_b[:, 0:2 * NODE_TILES * P].rearrange("p (s j c) -> p s j c", s=2, j=NODE_TILES)

        pair = ctx.enter_context(nc.psum_tensor("pair", [P, 2, BANK], F32))
        trio = ctx.enter_context(nc.psum_tensor("trio", [P, 2, 3, BANK], F32))

        edges_in, x_in, small_in = sem("edges_in"), sem("x_in"), sem("small_in")
        consts_made, counts_zeroed = sem("consts_made"), sem("counts_zeroed")
        keys_made, keys_turned, keys_kept = sem("keys_made"), sem("keys_turned"), sem("keys_kept")
        rows_made, rows_kept = sem("rows_made"), sem("rows_kept")
        main_hot, src_hot, ring_keyed = sem("main_hot"), sem("src_hot"), sem("ring_keyed")
        group_counted, group_added = sem("group_counted"), sem("group_added")
        far_hot, far_counted, far_added = sem("far_hot"), sem("far_counted"), sem("far_added")
        counts_done = sem("counts_done")
        degrees_ready, degrees_taken = sem("degrees_ready"), sem("degrees_taken")
        var_ready, std_ready, x_normed = sem("var_ready"), sem("std_ready"), sem("x_normed")
        h0_ready, h0_hi, h0_lo = sem("h0_ready"), sem("h0_hi"), sem("h0_lo")
        w_in, w_hi, w_used = sem("w_in"), sem("w_hi"), sem("w_used")
        max_local, max_over_all, scales_ready = sem("max_local"), sem("max_over_all"), sem("scales_ready")
        msg_ready, msg_hi, msg_split = sem("msg_ready"), sem("msg_hi"), sem("msg_split")
        root_ready, root_taken = sem("root_ready"), sem("root_taken")
        rel_ready, rel_taken, rel_added = sem("rel_ready"), sem("rel_taken"), sem("rel_added")
        h_scaled, h_hi, block_done = sem("h_scaled"), sem("h_hi"), sem("block_done")
        resid_in, out_turned, out_added, stored = sem("resid_in"), sem("out_turned"), sem("out_added"), sem("stored")
        bias_turned = sem("bias_turned")
        dve_step, far_step = sem("dve_step"), sem("far_step")

        def own_view(l, half):
            ks = 4 if half == 0 else K_TILES[l] - 4
            return ks, w_raw[:, 0:ks * MATS * P]

        block = ctx.enter_context(nc.Block())

        @block.sync
        def _(sp):
            for a, arr in enumerate((dst, src, edge_type)):
                sp.dma_start(ed[:, a], arr.rearrange("(h p i) -> p h i", h=HALVES, p=GP)
                             ).then_inc(edges_in, 16)
            for r in range(RELS):
                sp.dma_start(type_i[r:r + 1, :], node_type.rearrange("(a n) -> a n", a=1)
                             ).then_inc(small_in, 16)
            sp.dma_start(emb, node_emb).then_inc(small_in, 16)
            for l in range(LAYERS):
                sp.dma_start(bias_rows[FIRST[l]:FIRST[l] + T[l], :],
                             bias[l].rearrange("(t p) -> t p", p=P)).then_inc(small_in, 16)
            sp.dma_start(x_sb[:, 0:NODE_TILES - 1, :],
                         x[0:FULL_ROWS, :].rearrange("(j p) c -> p j c", p=P)).then_inc(x_in, 16)
            sp.dma_start(x_sb[0:LAST_ROWS, NODE_TILES - 1, :], x[FULL_ROWS:N, :]).then_inc(x_in, 16)

            def load_scan(l, kt, half):
                cols = T[l] * P
                for q in range(2):
                    sp.dma_start(w_raw[:, q * cols:(q + 1) * cols],
                                 mats[l][2 * half + q][bass.ds(kt * P, P), :]).then_inc(w_in, 16)

            def load_own(l, t, half):
                ks, raw = own_view(l, half)
                view = raw.rearrange("p (k m e) -> p k m e", k=ks, m=MATS)
                for m in range(MATS):
                    rows = mats[l][m][half * 4 * P:(half * 4 + ks) * P, bass.ds(t * P, P)]
                    sp.dma_start(view[:, :, m, :], rows.rearrange("(k p) e -> p k e", p=P)
                                 ).then_inc(w_in, 16)

            load_scan(0, 0, 0)
            for n in range(1, SCANS0):
                sp.wait_ge(w_used, n)
                load_scan(0, n // 2, n % 2)
            for half in range(2):
                sp.wait_ge(w_used, SCANS0 + half)
                load_own(0, 0, half)

            def block_loads(l, t, next_l, next_t):
                before = used_before(l, t)
                for half in range(scans(l)):
                    sp.wait_ge(w_used, before + half)
                    load_scan(l + 1, t, half)
                if l == LAST:
                    slot = sp.snap(t % 2)
                    sp.wait_ge(stored, 32 * t + STORE_CREDIT - 32)
                    sp.wait_ge(resid_in, 32 * t + RESID_CREDIT)
                    for j0, nj, rows in ((0, NODE_TILES - 1, P), (NODE_TILES - 1, 1, LAST_ROWS)):
                        sp.dma_start(
                            resid[0:rows, bass.ds(slot, 1), j0:j0 + nj, :].rearrange("p s j c -> p (s j) c"),
                            x[j0 * P:j0 * P + nj * rows, bass.ds(t * P, P)].rearrange("(j p) c -> p j c", p=rows)
                        ).then_inc(resid_in, 16)
                if next_l is not None:
                    for half in range(2):
                        sp.wait_ge(w_used, before + scans(l) + half)
                        load_own(next_l, next_t, half)

            for l in range(LAYERS):
                if l == LAST:
                    sp.wait_ge(root_ready, FIRST[LAST])
                with sp.Fori(0, T[l] - 1) as t:
                    block_loads(l, t, l, t + 1)
                block_loads(l, T[l] - 1, l + 1 if l < LAST else None, 0)

        @block.gpsimd
        def _(pool):
            pool.iota(iota_i, [[1, WIN_COLS]], base=0, channel_multiplier=0).then_inc(consts_made, 1)
            pool.iota(part_id_i, [[0, 1]], base=0, channel_multiplier=1).then_inc(consts_made, 1)
            pool.memset(ident[:], 1.0).then_inc(consts_made, 1)
            pool.wait_ge(consts_made, 3)
            pool.affine_select(out=ident[:], in_=ident[:], compare_op=ALU.is_equal, fill=0.0, base=0,
                               pattern=[[-1, P]], channel_multiplier=1).then_inc(consts_made, 1)
            pool.memset(ones_h, 1.0).then_inc(consts_made, 1)
            pool.memset(counts[:, NODE_TILES // 2:], 0.0).then_inc(counts_zeroed, 1)

            def join(n):
                pool.wait_ge(max_local, n)
                pool.partition_all_reduce(over_all[:], local[:], P, RMAX).then_inc(max_over_all, 1)

            join(1)
            pool.wait_ge(keys_kept, 2)
            with pool.Fori(0, GROUPS // RING) as it:
                pool.wait_ge(src_hot, it * RING + SRC_CREDIT)
                pool.tensor_copy(ring_keys, keys_t[:, 1, :, bass.ds(it * RING, RING)]).then_inc(ring_keyed, 1)
                pool.wait_ge(ring_keyed, it + 1)
                pool.tensor_tensor(gate[:, RING:RING + 1], ident[0:SUB, 0:1], ident[0:SUB, 0:1], ALU.mult)
                for slot in range(RING):
                    g = it * RING + slot
                    pool.wait_ge(group_counted, g + RING_CREDIT - RING + 1)
                    pool.tensor_tensor(gate[:, slot:slot + 1], ident[0:SUB, 0:1], ident[0:SUB, 0:1], ALU.mult)
                    for u in range(SUBS):
                        last = pool.tensor_scalar(ring_src[0:SUB, slot, u, :], iota_h[0:SUB, 0:P],
                                                  ring_keys[:, u, slot:slot + 1], None, ALU.is_equal)
                    last.then_inc(src_hot, 1)
            for n in range(2, 7):
                join(n)

        @block.scalar
        def _(act):
            act.wait_ge(var_ready, 1)
            nc.scalar.activation(std, var_eps, ACT.Sqrt).then_inc(std_ready, 1)
            for k in range(K_TILES[0]):
                act.wait_ge(h0_ready, k + 1)
                for c, (c0, cw) in enumerate(H0_CHUNKS):
                    last = nc.scalar.activation(h_a[:, 0, k, c0:c0 + cw], trio[:, k % 2, c, 0:cw],
                                                ACT.Relu if k < IN_CH // P else ACT.Copy)
                last.then_inc(h0_hi, 1)

            def split_w(l, t, half, in_count):
                ks, raw = own_view(l, half)
                act.wait_ge(w_in, in_count)
                nc.scalar.activation(
                    w_split[:, 4 * half:4 * half + ks, 0].rearrange("p k m e -> p k (m e)"),
                    raw.rearrange("p (k e) -> p k e", k=ks), ACT.Copy, scale=sc[:, l, W_SCALE:W_SCALE + 1]
                ).then_inc(w_hi, 1)

            act.wait_ge(scales_ready, w_scaled_at(0))
            act.wait_ge(counts_done, 1)
            act.wait_ge(degrees_ready, RELS)
            split_w(0, 0, 0, SCANS0 * SCAN_INC + OWN_INC)
            split_w(0, 0, 1, IN0)

            def store(t):
                act.wait_ge(out_added, t + 1)
                act.wait_ge(stored, 32 * t + STORE_CREDIT)
                slot = act.snap(t % 2)
                for j0, nj, rows in ((0, NODE_TILES - 1, P), (NODE_TILES - 1, 1, LAST_ROWS)):
                    act.dma_start(
                        out[j0 * P:j0 * P + nj * rows, bass.ds(t * P, P)].rearrange("(j p) c -> p j c", p=rows),
                        resid[0:rows, bass.ds(slot, 1), j0:j0 + nj, :].rearrange("p s j c -> p (s j) c")
                    ).then_inc(stored, 16)

            def act_block(l, t, next_l, next_t, stores):
                g = FIRST[l] + t
                for j in range(NODE_TILES):
                    rows = P if j < NODE_TILES - 1 else LAST_ROWS
                    act.wait_ge(msg_ready, NODE_TILES * g + j + 1)
                    nc.scalar.activation(msg[0:rows, j, 0, :], pair[0:rows, j % 2, 0:RELS * P], ACT.Copy,
                                         scale=sc[0:rows, l, M_SCALE:M_SCALE + 1]).then_inc(msg_hi, 1)
                if stores:
                    store(t - 1)
                act.wait_ge(root_ready, g + 1)
                if l < LAST:
                    act.wait_ge(block_done, g + DONE_CREDIT)
                for c, (c0, cw) in enumerate(CHUNKS):
                    last = nc.scalar.activation(acc[:, c0:c0 + cw], trio[:, 0, c, 0:cw], ACT.Identity,
                                                bias=bias_sb[:, bass.ds(g, 1)],
                                                scale=sc[:, l, ROOT_BACK:ROOT_BACK + 1])
                last.then_inc(root_taken, 1)
                if next_l is not None:
                    act.wait_ge(scales_ready, w_scaled_at(next_l))
                    for half in range(2):
                        split_w(next_l, next_t, half,
                                in_before(l, t) + scans(l) * SCAN_INC + (half + 1) * OWN_INC)
                if l < LAST:
                    act.wait_ge(h_scaled, g + 1)
                    nc.scalar.activation(h_in[l + 1][:, 0, bass.ds(t, 1), :].rearrange("p k n -> p (k n)"),
                                         acc[:], ACT.Copy).then_inc(h_hi, 1)

            for l in range(LAYERS):
                act.wait_ge(scales_ready, m_scaled_at(l))
                if l == LAST:
                    act.wait_ge(block_done, FIRST[LAST] + DONE_CREDIT)
                    act_block(l, 0, l, 1, False)
                with act.Fori(1 if l == LAST else 0, T[l] - 1) as t:
                    act_block(l, t, l, t + 1, l == LAST)
                act_block(l, T[l] - 1, l + 1 if l < LAST else None, 0, l == LAST)
            store(T[LAST] - 1)
            act.wait_ge(stored, 32 * T[LAST] + STORE_CREDIT)

        @block.vector
        def _(dve):
            steps = Steps(dve, dve_step)
            then = steps.then
            V = nc.vector

            V.memset(counts[:, 0:NODE_TILES // 2], 0.0).then_inc(counts_zeroed, 1)

            dve.wait_ge(edges_in, 48)
            d_i = ed[:, 0]
            src_f = ed[:, 1].rearrange("p h i -> p (h i)")
            rel_f = ed[:, 2].rearrange("p h i -> p (h i)")
            flat = [keys[:, a].rearrange("p h u i -> p (h u i)") for a in range(4)]
            V.tensor_scalar(src_hi, src_f, 7, None, ALU.logical_shift_right)
            V.tensor_scalar(src_lo, src_f, P - 1, None, ALU.bitwise_and)
            V.tensor_reduce(highest, d_i, AX.X, ALU.max)
            then(V.tensor_reduce(lowest, d_i, AX.X, ALU.min))
            for h in range(HALVES):
                V.tensor_scalar(keys[:, 3, h].rearrange("p u i -> p (u i)"), d_i[:, h, :], lowest[:, h:h + 1],
                                None, ALU.subtract)
            V.tensor_copy(flat[1], src_lo)
            V.tensor_tensor(extra, highest, lowest, ALU.subtract)
            then(V.tensor_scalar(key_tmp, rel_f, float(WIN), 1.0, ALU.mult, ALU.add))
            then(V.scalar_tensor_tensor(out=flat[2], in0=src_hi, scalar=float(RELS * WIN), in1=key_tmp,
                                        op0=ALU.mult, op1=ALU.add))
            then(V.tensor_scalar(extra, extra, 0.5, 1.0 / WIN, ALU.add, ALU.mult))
            then(V.tensor_scalar(extra, extra, -0.5, None, ALU.add))
            then(V.tensor_tensor(key_tmp, flat[2], flat[3], ALU.add))
            then(V.scalar_tensor_tensor(out=key_tmp, in0=flat[3], scalar=float(WIN), in1=key_tmp,
                                        op0=ALU.is_lt, op1=ALU.mult))
            V.tensor_scalar(flat[0], key_tmp, -1.0, None, ALU.add).then_inc(keys_made, 1)

            dve.wait_ge(small_in, 16 * (RELS + 1 + LAYERS))
            dve.wait_ge(consts_made, 5)
            dve.wait_ge(bias_turned, 1)
            then(V.tensor_copy(bias_sb[:], pair[:, 1, 0:BLOCKS]))
            V.tensor_copy(iota_h, iota_i)
            V.tensor_copy(part_id, part_id_i)
            then(V.memset(local[:], 0.0))
            V.tensor_reduce(local[0:RELS, 0:1], emb, AX.X, ALU.max, apply_absolute_value=True)
            V.tensor_reduce(local[:, 1:2], bias_sb[:], AX.X, ALU.max,
                            apply_absolute_value=True).then_inc(max_local, 1)

            def c_(l, k):
                return sc[:, l, k:k + 1]

            def scale_of(l, bound, scale, back):
                then(V.tensor_scalar(c_(l, back).bitcast(I32), c_(l, bound).bitcast(I32), EXPONENT, None,
                                     ALU.bitwise_and))
                then(V.tensor_scalar(c_(l, scale).bitcast(I32), c_(l, back).bitcast(I32), -1.0, INVERSE_BITS,
                                     ALU.mult, ALU.add))
                V.tensor_scalar(c_(l, scale), c_(l, scale), TOP, None, ALU.mult)
                return V.tensor_scalar(c_(l, back), c_(l, back), 1.0 / TOP, None, ALU.mult)

            dve.wait_ge(max_over_all, 1)
            V.tensor_copy(bias_max[:], over_all[:, 1:2])
            then(V.tensor_scalar(c_(0, B1), over_all[:, 0:1], LN_BOUND, None, ALU.max))
            then(scale_of(0, B1, H_SCALE, H_BACK))
            then(V.tensor_tensor(c_(0, H_TOP), c_(0, B1), c_(0, H_SCALE), ALU.mult))
            V.tensor_copy(local[:, 0:1], c_(0, H_TOP)).then_inc(scales_ready, 1)
            V.tensor_scalar(hot_type, type_i, part_id[0:RELS], c_(0, H_SCALE)[0:RELS],
                            ALU.is_equal, ALU.mult).then_inc(x_normed, 1)

            dve.wait_ge(x_in, 32)
            for j in range(NODE_TILES):
                rows = P if j < NODE_TILES - 1 else LAST_ROWS
                for s in range(2):
                    V.bn_stats(stats[0:rows, j, 6 * s:6 * s + 6], x_sb[0:rows, j, 384 * s:384 * s + 384])
            if LAST_ROWS < P:
                V.memset(mean_var[:, NODE_TILES - 1, :], 1.0)
            then(V.tensor_copy(local[:, 1:2], bias_max[:]))
            for j in range(NODE_TILES):
                rows = P if j < NODE_TILES - 1 else LAST_ROWS
                ins = V.bn_aggr(mean_var[0:rows, j, :], stats[0:rows, j, :])
            then(ins)
            V.tensor_scalar(var_eps, mean_var[:, :, 1], EPS, None, ALU.add).then_inc(var_ready, 1)
            dve.wait_ge(std_ready, 1)
            then(V.reciprocal(rstd, std))
            then(V.tensor_tensor(newton, rstd, rstd, ALU.mult))
            then(V.tensor_tensor(newton2, newton, var_eps, ALU.mult))
            then(V.tensor_scalar(newton, newton2, -0.5, 1.5, ALU.mult, ALU.add))
            then(V.tensor_tensor(newton2, newton, rstd, ALU.mult))
            then(V.tensor_scalar(rstd, newton2, c_(0, H_SCALE), None, ALU.mult))
            for j in range(NODE_TILES):
                rows = P if j < NODE_TILES - 1 else LAST_ROWS
                ins = V.tensor_scalar(x_sb[0:rows, j, :], x_sb[0:rows, j, :], mean_var[0:rows, j, 0:1],
                                      rstd[0:rows, j:j + 1], ALU.subtract, ALU.mult)
            ins.then_inc(x_normed, 1)

            for a in range(4):
                dve.wait_ge(keys_turned, a + 1)
                V.tensor_copy(keys_t[:, a], trio[0:SUB, a % 2, a // 2, 0:SUBS * GROUPS].rearrange(
                    "p (u g) -> p u g", u=SUBS)).then_inc(keys_kept, 1)
            dve.wait_ge(rows_made, 1)
            then(V.tensor_copy(row_f, pair[0:1, 0, 0:2 * GROUPS].rearrange("p (a g) -> p a g", a=2)))
            V.tensor_copy(row_i, row_f[:, 0, :])
            then(V.tensor_reduce(most_f, row_f[:, 1, :], AX.X, ALU.max))
            V.tensor_copy(most_i, most_f).then_inc(rows_kept, 1)

            for k in range(K_TILES[0]):
                dve.wait_ge(h0_hi, k + 1)
                for c, (c0, cw) in enumerate(H0_CHUNKS):
                    if k < IN_CH // P:
                        ins = V.scalar_tensor_tensor(out=h_a[:, 1, k, c0:c0 + cw], in0=trio[:, k % 2, c, 0:cw],
                                                     scalar=0.0, in1=h_a[:, 0, k, c0:c0 + cw],
                                                     op0=ALU.max, op1=ALU.subtract)
                    else:
                        ins = V.tensor_tensor(h_a[:, 1, k, c0:c0 + cw], trio[:, k % 2, c, 0:cw],
                                              h_a[:, 0, k, c0:c0 + cw], ALU.subtract)
                ins.then_inc(h0_lo, 1)

            def hot_rows(g, slot):
                dve.wait_ge(group_counted, g + RING_CREDIT - RING + 1)
                for u in range(SUBS):
                    ins = V.tensor_scalar(ring_main[0:SUB, slot, u, :], iota_h[0:SUB, :],
                                          keys_t[:, 0, u, bass.ds(g, 1)], None, ALU.is_equal)
                ins.then_inc(main_hot, 1)

            def add_window(bank, first):
                view = counts[:, :, :, bass.ds(first, WIN)]
                return V.tensor_tensor(view, view, pair[:, bank, 0:WIN_COLS].rearrange(
                    "p (j r d) -> p j r d", j=NODE_TILES, r=RELS), ALU.add)

            def add_group(g, bank):
                first = dve.value_load(row_i[0:1, bass.ds(g, 1)], min_val=0, max_val=N - 1)
                dve.wait_ge(group_counted, g + RING_CREDIT + 1)
                dve.wait_ge(group_added, g + BANK_CREDIT)
                add_window(bank, first).then_inc(group_added, 1)

            def scan(in_count, cols, at):
                dve.wait_ge(w_in, in_count)
                V.tensor_reduce(tile_max[:, at:at + 1] if isinstance(at, int) else tile_max[:, bass.ds(at, 1)],
                                w_raw[:, 0:2 * cols], AX.X, ALU.max,
                                apply_absolute_value=True).then_inc(w_used, 1)

            dve.wait_ge(counts_zeroed, 2)
            for slot in range(RING):
                hot_rows(slot, slot)
            scan(SCAN_INC, T[0] * P, 0)
            dve.wait_ge(rows_kept, 1)
            with dve.Fori(0, SCANS0 - 1) as it:
                for q in range(SCAN_EVERY):
                    g = it * SCAN_EVERY + q
                    add_group(g, q % 2)
                    hot_rows(g + RING, q % RING)
                scan(SCAN_INC * (it + 2), T[0] * P, it + 1)
            for slot in range(RING):
                add_group(GROUPS - RING + slot, slot % 2)

            most = dve.value_load(most_i, min_val=0, max_val=N // WIN)
            with dve.If(most > 0):
                dve.wait_ge(group_added, GROUPS + BANK_CREDIT)
                far_steps = Steps(dve, far_step)
                with dve.Fori(0, GROUPS) as g:
                    first = dve.value_load(row_i[0:1, bass.ds(g, 1)], min_val=0, max_val=N - 1)
                    with dve.Fori(1, most + 1) as s:
                        v = dve.snap(g * most + s)
                        start = dve.snap((first + s * WIN) % (LAST_WIN + 1))
                        shift, rel, inside, key = far[:, 0:1], far[:, 1:3], far[:, 3:5], far[:, 5:7]
                        far_steps.base, far_steps.count = (v - 1) * FAR_STEPS, 0
                        fthen = far_steps.then
                        fthen(V.tensor_scalar(shift, iota_i[0:SUB, bass.ds(s, 1)], float(WIN), None, ALU.mult))
                        fthen(V.tensor_scalar(rel, keys_t[:, 3, :, bass.ds(g, 1)].rearrange("p u g -> p (u g)"),
                                              shift, None, ALU.subtract))
                        fthen(V.tensor_scalar(inside, rel, 0.0, None, ALU.is_ge))
                        fthen(V.tensor_tensor(key, keys_t[:, 2, :, bass.ds(g, 1)].rearrange("p u g -> p (u g)"),
                                              rel, ALU.add))
                        fthen(V.tensor_tensor(key, key, inside, ALU.mult))
                        fthen(V.scalar_tensor_tensor(out=key, in0=rel, scalar=float(WIN), in1=key,
                                                     op0=ALU.is_lt, op1=ALU.mult))
                        fthen(V.tensor_scalar(key, key, -1.0, None, ALU.add))
                        for u in range(SUBS):
                            V.tensor_scalar(ring_main[0:SUB, 0, u, :], iota_h[0:SUB, :], key[:, u:u + 1],
                                            None, ALU.is_equal)
                            ins = V.tensor_scalar(ring_src[0:SUB, 0, u, :], iota_h[0:SUB, 0:P],
                                                  keys_t[:, 1, u, bass.ds(g, 1)], None, ALU.is_equal)
                        ins.then_inc(far_hot, 1)
                        dve.wait_ge(far_counted, v)
                        add_window(0, start).then_inc(far_added, 1)
                        dve.wait_ge(far_added, v)

            dve.wait_ge(group_added, GROUPS + BANK_CREDIT)
            V.memset(local[:, 1:2], 0.0).then_inc(counts_done, 1)

            def joined(n, column, maxima):
                V.tensor_reduce(local[:, column:column + 1], maxima, AX.X, ALU.max).then_inc(max_local, 1)
                dve.wait_ge(max_over_all, n)

            def weight_scales(l, n):
                dve.wait_ge(w_used, used_before(l - 1, T[l - 1] - 1) + 2 if l else SCANS0)
                joined(n, 0, tile_max[:, 0:SCANS0 if l == 0 else 2 * K_TILES[l]])
                then(V.tensor_scalar(c_(l, W_MAX), over_all[:, 0:1], TINY, None, ALU.max))
                scale_of(l, W_MAX, W_SCALE, W_BACK).then_inc(scales_ready, 1)

            def message_scales(l):
                dve.wait_ge(scales_ready, w_scaled_at(l))
                then(V.tensor_tensor(c_(l, B1), c_(l, W_MAX), c_(l, W_SCALE), ALU.mult))
                then(V.tensor_tensor(c_(l, B1), c_(l, B1), c_(l, H_TOP), ALU.mult))
                then(V.tensor_scalar(c_(l, B1), c_(l, B1), K_BOUND, TINY, ALU.mult, ALU.max))
                then(scale_of(l, B1, M_SCALE, M_BACK))
                then(V.tensor_tensor(c_(l, ROOT_BACK), c_(l, H_BACK), c_(l, W_BACK), ALU.mult))
                ins = V.tensor_tensor(c_(l, REL_BACK), c_(l, ROOT_BACK), c_(l, M_BACK), ALU.mult)
                if l < LAST:
                    then(ins)
                    then(V.tensor_tensor(c_(l + 1, B2), c_(l, H_TOP), c_(l, H_BACK), ALU.mult))
                    then(V.tensor_tensor(c_(l + 1, B2), c_(l + 1, B2), c_(l, W_MAX), ALU.mult))
                    then(V.tensor_scalar(c_(l + 1, B2), c_(l + 1, B2), MATS * K_BOUND, bias_max[:],
                                         ALU.mult, ALU.add))
                    then(V.tensor_scalar(c_(l + 1, B2), c_(l + 1, B2), TINY, None, ALU.max))
                    ins = scale_of(l + 1, B2, H_SCALE, H_BACK)
                ins.then_inc(scales_ready, 1)
                dve.wait_ge(scales_ready, m_scaled_at(l))

            for r in range(RELS):
                dve.wait_ge(degrees_ready, r + 1)
                for c, (c0, cw) in enumerate(CHUNKS):
                    ins = V.tensor_scalar(inv[:, r, c0:c0 + cw], trio[:, r % 2, c, 0:cw], 1.0, None, ALU.max)
                ins.then_inc(degrees_taken, 1)
                dve.wait_ge(degrees_taken, r + 1)
                ins = V.reciprocal(inv[:, r, :], inv[:, r, :])
            then(ins)
            weight_scales(0, 2)
            message_scales(0)

            def low_w(l, half, nth_hi):
                ks, raw = own_view(l, half)
                dve.wait_ge(w_hi, nth_hi)
                to = w_split[:, 4 * half:4 * half + ks]
                V.scalar_tensor_tensor(out=to[:, :, 1].rearrange("p k m e -> p k (m e)"),
                                       in0=raw.rearrange("p (k e) -> p k e", k=ks), scalar=c_(l, W_SCALE),
                                       in1=to[:, :, 0].rearrange("p k m e -> p k (m e)"),
                                       op0=ALU.mult, op1=ALU.subtract).then_inc(w_used, 1)

            for half in range(2):
                low_w(0, half, half + 1)

            def add_relation(l, g, r):
                dve.wait_ge(rel_ready, RELS * g + r + 1)
                for c, (c0, cw) in enumerate(CHUNKS):
                    nth = 9 * g + 3 * r + c
                    V.scalar_tensor_tensor(out=part[:, 0:cw], in0=trio[:, (r + 1) % 2, c, 0:cw],
                                           scalar=c_(l, REL_BACK), in1=inv[:, r, c0:c0 + cw],
                                           op0=ALU.mult, op1=ALU.mult).then_inc(rel_taken, 1)
                    dve.wait_ge(rel_taken, nth + 1 + SLOT_CREDIT)
                    if r == 0 and c == 0:
                        dve.wait_ge(root_taken, g + 1)
                    V.tensor_tensor(acc[:, c0:c0 + cw], acc[:, c0:c0 + cw], part[:, 0:cw],
                                    ALU.add).then_inc(rel_added, 1)
                    dve.wait_ge(rel_added, nth + 1)

            def add_residual(t):
                dve.wait_ge(out_turned, t + 1)
                dve.wait_ge(resid_in, 32 * (t + 1) + RESID_CREDIT)
                slot = dve.snap(t % 2)
                for bank, (j0, nj, rows) in enumerate(((0, 4, P), (4, 4, P), (8, 1, P), (9, 1, LAST_ROWS))):
                    view = resid[0:rows, bass.ds(slot, 1), j0:j0 + nj, :].rearrange("p s j c -> p (s j c)")
                    at = (j0 % 4) * P
                    ins = V.tensor_tensor(view, view, trio[0:rows, 0, j0 // 4, at:at + nj * P], ALU.add)
                ins.then_inc(out_added, 1)

            def dve_block(l, t, next_l, adds):
                g = FIRST[l] + t
                for j in range(NODE_TILES):
                    rows = P if j < NODE_TILES - 1 else LAST_ROWS
                    dve.wait_ge(msg_hi, NODE_TILES * g + j + 1)
                    V.scalar_tensor_tensor(out=msg[0:rows, j, 1, :], in0=pair[0:rows, j % 2, 0:RELS * P],
                                           scalar=c_(l, M_SCALE)[0:rows], in1=msg[0:rows, j, 0, :],
                                           op0=ALU.mult, op1=ALU.subtract).then_inc(msg_split, 1)
                    if l < LAST and j in (3, 7):
                        half = j // 4
                        scan(in_before(l, t) + (half + 1) * SCAN_INC, T[l + 1] * P, 2 * t + half)
                if l < LAST and next_l == l + 1:
                    weight_scales(l + 1, 3 + 2 * l)
                if adds:
                    add_residual(t - 1)
                for r in range(RELS):
                    if next_l is not None and r < 2:
                        low_w(next_l, r, 2 * g + 2 + r + 1)
                    add_relation(l, g, r)
                if l == LAST:
                    V.tensor_scalar(acc[:], acc[:], 0.0, None, ALU.max).then_inc(h_scaled, 1)
                    return
                V.tensor_scalar(acc[:], acc[:], 0.0, c_(l + 1, H_SCALE), ALU.max,
                                ALU.mult).then_inc(h_scaled, 1)
                dve.wait_ge(h_scaled, g + 1)
                V.tensor_reduce(tile_max[:, bass.ds(SCANS0 + t, 1)], acc[:], AX.X, ALU.max)
                dve.wait_ge(h_hi, g + 1)
                to = h_in[l + 1]
                V.tensor_tensor(to[:, 1, bass.ds(t, 1), :].rearrange("p k n -> p (k n)"), acc[:],
                                to[:, 0, bass.ds(t, 1), :].rearrange("p k n -> p (k n)"),
                                ALU.subtract).then_inc(block_done, 1)

            for l in range(LAYERS):
                if l:
                    dve.wait_ge(block_done, FIRST[l] + DONE_CREDIT)
                    joined(2 + 2 * l, 1, tile_max[:, SCANS0:SCANS0 + T[l - 1]])
                    then(V.tensor_copy(c_(l, H_TOP), over_all[:, 1:2]))
                    message_scales(l)
                if l == LAST:
                    dve_block(l, 0, l, False)
                with dve.Fori(1 if l == LAST else 0, T[l] - 1) as t:
                    dve_block(l, t, l, l == LAST)
                dve_block(l, T[l] - 1, l + 1 if l < LAST else None, l == LAST)
            add_residual(T[LAST] - 1)

        @block.tensor
        def _(pe):
            M = nc.tensor
            pe.sem_inc(group_counted, RING_CREDIT)
            pe.sem_inc(group_added, BANK_CREDIT)
            pe.sem_inc(msg_split, BANK_CREDIT)
            pe.sem_inc(rel_taken, SLOT_CREDIT)
            pe.sem_inc(stored, STORE_CREDIT)
            pe.sem_inc(resid_in, RESID_CREDIT)
            pe.sem_inc(block_done, DONE_CREDIT)
            pe.sem_inc(src_hot, SRC_CREDIT)

            pe.wait_ge(consts_made, 5)
            pe.wait_ge(small_in, 16 * (RELS + 1 + LAYERS))
            M.transpose(pair[:, 1, 0:BLOCKS], bias_rows, ident[0:BLOCKS, 0:BLOCKS]).then_inc(bias_turned, 1)
            pe.wait_ge(keys_made, 1)
            for a in range(4):
                for u in range(SUBS):
                    for h in range(HALVES):
                        at = u * GROUPS + h * GP
                        last = M.transpose(trio[0:SUB, a % 2, a // 2, at:at + GP], keys[:, a, h, u, :],
                                           ident[0:GP, 0:GP])
                last.then_inc(keys_turned, 1)
            for a, col in enumerate((lowest, extra)):
                for h in range(HALVES):
                    at = a * GROUPS + h * GP
                    last = M.matmul(pair[0:1, 0, at:at + GP], col[:, h:h + 1], ident[0:GP, 0:GP],
                                    start=True, stop=True, skip_group_check=True)
            last.then_inc(rows_made, 1)

            pe.wait_ge(keys_kept, 4)
            pe.wait_ge(x_normed, 2)
            for k in range(K_TILES[0]):
                if k >= 2:
                    pe.wait_ge(h0_lo, k - 1)
                if k < IN_CH // P:
                    for j in range(NODE_TILES):
                        rows = P if j < NODE_TILES - 1 else LAST_ROWS
                        at = (j % 4) * P
                        last = M.transpose(trio[:, k % 2, j // 4, at:at + rows],
                                           x_sb[0:rows, j, k * P:(k + 1) * P], ident[0:rows, 0:rows])
                else:
                    for c, (c0, cw) in enumerate(H0_CHUNKS):
                        last = M.matmul(trio[:, k % 2, c, 0:cw], emb, hot_type[:, c0:c0 + cw],
                                        start=True, stop=True)
                last.then_inc(h0_ready, 1)

            def count(slot, bank):
                for u in range(SUBS):
                    ins = M.matmul(pair[:, bank, 0:WIN_COLS], ring_src[0:SUB, slot, u, :],
                                   ring_main[0:SUB, slot, u, :], start=(u == 0), stop=(u == SUBS - 1))
                return ins

            pe.wait_ge(rows_kept, 1)
            with pe.Fori(0, GROUPS // RING) as it:
                for slot in range(RING):
                    g = it * RING + slot
                    pe.wait_ge(main_hot, g + 1)
                    pe.wait_ge(src_hot, g + 1 + SRC_CREDIT)
                    pe.wait_ge(group_added, g + BANK_CREDIT - 1)
                    count(slot, slot % 2).then_inc(group_counted, 1)
            most = pe.value_load(most_i, min_val=0, max_val=N // WIN)
            with pe.If(most > 0):
                with pe.Fori(0, GROUPS * most) as v:
                    pe.wait_ge(far_hot, v + 1)
                    count(0, 0).then_inc(far_counted, 1)

            pe.wait_ge(counts_done, 1)
            pe.wait_ge(h0_lo, K_TILES[0])
            for r in range(RELS):
                if r == 2:
                    pe.wait_ge(degrees_taken, 1)
                for j in range(NODE_TILES):
                    for c, (c0, cw) in enumerate(CHUNKS):
                        last = M.matmul(trio[:, r % 2, c, 0:cw], ones_h, counts[:, j, r, c0:c0 + cw],
                                        start=(j == 0), stop=(j == NODE_TILES - 1))
                last.then_inc(degrees_ready, 1)

            def messages(l, g, j, bank, rows, w_count):
                pe.wait_ge(msg_split, NODE_TILES * g + j - 1 + BANK_CREDIT)
                pe.wait_ge(w_used, w_count)
                to = pair[0:rows, bank, 0:RELS * P]
                for k in range(K_TILES[l]):
                    for n, (ph, pw) in enumerate(((0, 0), (0, 1), (1, 0))):
                        h_tile = h_in[l][:, ph, k, bass.ds(j * P, rows)]
                        last = M.matmul(to, h_tile, w_split[:, k, pw, 0:RELS, :].rearrange("p m e -> p (m e)"),
                                        start=(k == 0 and n == 0), stop=(k == K_TILES[l] - 1 and n == 2))
                last.then_inc(msg_ready, 1)

            def root(l):
                for k in range(K_TILES[l]):
                    for n, (pw, ph) in enumerate(((0, 0), (0, 1), (1, 0))):
                        for c, (c0, cw) in enumerate(CHUNKS):
                            last = M.matmul(trio[:, 0, c, 0:cw], w_split[:, k, pw, RELS, :],
                                            h_in[l][:, ph, k, c0:c0 + cw],
                                            start=(k == 0 and n == 0), stop=(k == K_TILES[l] - 1 and n == 2))
                return last

            def gather_tile(r, j, rows, start, stop):
                for pm in range(2):
                    for c, (c0, cw) in enumerate(CHUNKS):
                        last = M.matmul(trio[:, (r + 1) % 2, c, 0:cw],
                                        msg[0:rows, bass.ds(j, 1), pm, r * P:(r + 1) * P].rearrange("p j e -> p (j e)"),
                                        counts[0:rows, bass.ds(j, 1), r, c0:c0 + cw].rearrange("p j n -> p (j n)"),
                                        start=start and pm == 0, stop=stop and pm == 1)
                return last

            def turn_out(t):
                pe.wait_ge(h_scaled, FIRST[LAST] + t + 1)
                pe.wait_ge(rel_taken, 9 * (FIRST[LAST] + t + 1) - 3 + SLOT_CREDIT)
                for j in range(NODE_TILES):
                    rows = P if j < NODE_TILES - 1 else LAST_ROWS
                    at = (j % 4) * P
                    last = M.transpose(trio[0:rows, 0, j // 4, at:at + P], acc[:, j * P:j * P + rows], ident[:])
                last.then_inc(out_turned, 1)

            def pe_block(l, t, turns):
                g = FIRST[l] + t
                w_count = used_before(l, t)
                with pe.Fori(0, NODE_TILES // 2 - 1) as jj:
                    for bank in range(2):
                        messages(l, g, 2 * jj + bank, bank, P, w_count)
                messages(l, g, NODE_TILES - 2, 0, P, w_count)
                messages(l, g, NODE_TILES - 1, 1, LAST_ROWS, w_count)
                if turns:
                    turn_out(t - 1)
                    pe.wait_ge(out_added, t)
                pe.wait_ge(rel_taken, 9 * g - 3 + SLOT_CREDIT)
                root(l).then_inc(root_ready, 1)
                pe.wait_ge(msg_split, NODE_TILES * (g + 1) + BANK_CREDIT)
                for r in range(RELS):
                    if r == 1:
                        pe.wait_ge(root_taken, g + 1)
                    else:
                        pe.wait_ge(rel_taken, 9 * g + (3 if r == 2 else 0) + SLOT_CREDIT)
                    gather_tile(r, 0, P, True, False)
                    with pe.Fori(1, NODE_TILES - 1, 2) as j:
                        gather_tile(r, j, P, False, False)
                        gather_tile(r, j + 1, P, False, False)
                    gather_tile(r, NODE_TILES - 1, LAST_ROWS, False, True).then_inc(rel_ready, 1)

            pe.wait_ge(degrees_taken, RELS)
            for l in range(LAYERS):
                if l:
                    pe.wait_ge(block_done, FIRST[l] + DONE_CREDIT)
                if l == LAST:
                    pe_block(l, 0, False)
                with pe.Fori(1 if l == LAST else 0, T[l]) as t:
                    pe_block(l, t, l == LAST)
            turn_out(T[LAST] - 1)


_INS = ['x', 'src', 'dst', 'edge_type_3', 'node_type_3', 'L0_gnn_node_emb', 'L0_gnn_w_rel1', 'L0_gnn_w_root1',
        'L0_gnn_b1', 'L0_gnn_w_rel2', 'L0_gnn_w_root2', 'L0_gnn_b2', 'L0_gnn_w_rel3', 'L0_gnn_w_root3', 'L0_gnn_b3']
_OUTS = [((N, 768), 'float32')]


def kernel(**inputs):
    import numpy as _np
    import concourse.bacc as _bacc
    from concourse import mybir as _mybir
    from concourse.bass_utils import run_bass_kernel_spmd as _run

    nc = _bacc.Bacc("TRN2", target_bir_lowering=False, num_devices=1)
    arrays, args = {}, []
    for name in _INS:
        a = _np.ascontiguousarray(inputs[name])
        arrays[f"in_{name}_dram"] = a
        args.append(nc.dram_tensor(f"in_{name}_dram", a.shape, _mybir.dt.from_np(a.dtype), kind="ExternalInput").ap())
    for i, (shape, dtype) in enumerate(_OUTS):
        dt = _mybir.dt.from_np(_np.dtype(dtype))
        args.append(nc.dram_tensor(f"out_{i}_dram", shape, dt, kind="ExternalOutput").ap())
    gnn_kernel(nc, *args)
    r = _run(nc, [arrays], core_ids=[0])
    got = tuple(r.results[0][f"out_{i}_dram"] for i in range(len(_OUTS)))
    return got[0]
```

```python
from contextlib import ExitStack

import concourse.bass as bass
from concourse import mybir


P = 128
N = 1250
NODE_TILES = (N + P - 1) // P
FULL_ROWS = (NODE_TILES - 1) * P
LAST_ROWS = N - FULL_ROWS
IN_CH = 768
TYPE_DIM = 128
RELS = 3
MATS = RELS + 1
EDGES = 40000
K_TILES = (7, 7, 6)
T = (7, 6, 6)
LAYERS = 3
FIRST = (0, T[0], T[0] + T[1])
BLOCKS = sum(T)

CHUNKS = ((0, 417), (417, 417), (834, 416))
CHUNK = 417
BANK = 512
H0_CHUNKS = tuple((c, min(BANK, N - c)) for c in range(0, N, BANK))

SUB = 125
SUBS = 2
GROUPS = EDGES // (SUB * SUBS)
HALVES = 2
GP = GROUPS // HALVES
HE = EDGES // GP
WIN = 12
WIN_COLS = NODE_TILES * RELS * WIN
N_PAD = 1264
LAST_WIN = N_PAD - WIN
RING = 4
FAR_STEPS = 7
SCANS0 = K_TILES[0]
EARLY = 2
ROUNDS = GROUPS // RING
ROUNDS_FIRST = 3
ROUNDS_SPLIT = 2
EARLY_ROUNDS = NODE_TILES + K_TILES[0] + ROUNDS_SPLIT

TINY = 1e-30
EXPONENT = 0x7F800000
INVERSE_BITS = float(254 << 23)
TOP = 2.0 ** 14
K_BOUND = 1024.0
LN_BOUND = 27.8
EPS = 1e-5

F32 = mybir.dt.float32
F16 = mybir.dt.float16
I32 = mybir.dt.int32
ALU = mybir.AluOpType
ACT = mybir.ActivationFunctionType
AX = mybir.AxisListType
RMAX = bass.bass_isa.ReduceOp.max

RING_CREDIT = RING
BANK_CREDIT = 2
SLOT_CREDIT = 4
STORE_CREDIT = 64
RESID_CREDIT = 32
DONE_CREDIT = 1
SRC_CREDIT = 1

SCAN_INC = 2 * 16
OWN_INC = MATS * 16
OWN0 = 2
IN0 = 2 * OWN_INC
LAST = LAYERS - 1
START = (EARLY, 0, 1)


def used_before(l, t):
    return OWN0 + 4 * (FIRST[l] + t) if l < LAST else OWN0 + 4 * FIRST[l] + 2 * t


def in_before(l, t):
    block = 2 * (SCAN_INC + OWN_INC)
    return IN0 + block * (FIRST[l] + t) if l < LAST else IN0 + block * FIRST[l] + 2 * OWN_INC * t


def scans(l):
    return 2 if l < LAST else 0


def w_scaled_at(l):
    return 2 + 2 * l


def m_scaled_at(l):
    return 3 + 2 * l


class Steps:

    def __init__(self, eng, semaphore):
        self.eng, self.semaphore, self.base, self.count = eng, semaphore, 0, 0

    def then(self, instruction):
        self.count += 1
        instruction.then_inc(self.semaphore, 1)
        self.eng.wait_ge(self.semaphore, self.base + self.count)


def gnn_kernel(nc, x, src, dst, edge_type, node_type, node_emb,
               w_rel1, w_root1, b1, w_rel2, w_root2, b2, w_rel3, w_root3, b3, out):
    bias = (b1, b2, b3)
    mats = tuple([wr[0], wr[1], wr[2], wo] for wr, wo in
                 ((w_rel1, w_root1), (w_rel2, w_root2), (w_rel3, w_root3)))

    with ExitStack() as ctx:
        def sb(name, shape, dt):
            return ctx.enter_context(nc.sbuf_tensor(name, shape, dt))

        def sem(name):
            return ctx.enter_context(nc.semaphore(name))

        counts = sb("counts", [P, NODE_TILES, RELS, N_PAD], F16)
        h_a = sb("h_a", [P, 2, 7, N], F16)
        h_b = sb("h_b", [P, 2, 7, N], F16)
        h_in = (h_a, h_b, h_a)
        msg = sb("msg", [P, NODE_TILES, 2, RELS * P], F16)
        w_split = sb("w_split", [P, 7, 2, MATS, P], F16)
        w_raw = sb("w_raw", [P, 4 * MATS * P], F32)
        inv = sb("inv", [P, RELS, N], F32)
        acc = sb("acc", [P, N], F32)
        acc_b = sb("acc_b", [P, N], F32)
        ones_h = sb("ones_h", [P, P], F16)
        part = sb("part", [P, CHUNK], F32)
        ident = sb("ident", [P, P], F32)
        bias_sb = sb("bias_sb", [P, BLOCKS], F32)
        W_MAX, W_SCALE, W_BACK, H_TOP, H_SCALE, H_BACK, M_SCALE, M_BACK, ROOT_BACK, REL_BACK, B1, B2 = range(12)
        sc = sb("sc", [P, LAYERS, 12], F32)
        tile_max = sb("tile_max", [P, 3 * T[0]], F32)
        local = sb("local", [P, 2], F32)
        over_all = sb("over_all", [P, 2], F32)
        bias_max = sb("bias_max", [P, 1], F32)

        flat_a = h_a[:].rearrange("p a k n -> p (a k n)").bitcast(F32)
        flat_b = h_b[:].rearrange("p a k n -> p (a k n)").bitcast(F32)
        flat_w = w_split[:].rearrange("p k a m e -> p (k a m e)").bitcast(F32)
        flat_m = msg[:].rearrange("p j a e -> p (j a e)")
        flat_mf = flat_m.bitcast(F32)
        flat_i = inv[:].rearrange("p r n -> p (r n)")
        x_sb = flat_b[:, 0:NODE_TILES * IN_CH].rearrange("p (j c) -> p j c", j=NODE_TILES)

        def rows_of(k, n=1):
            return flat_a[0:GP, k * HE:(k + n) * HE]

        ed = rows_of(0, 3).bitcast(I32).rearrange("p (a h i) -> p a h i", a=3, h=HALVES)
        src_hi = rows_of(3).bitcast(I32)
        src_lo = rows_of(4).bitcast(I32)
        keys = rows_of(5, 4).rearrange("p (a h u i) -> p a h u i", a=4, h=HALVES, u=SUBS)
        key_tmp = rows_of(9)
        lowest = flat_a[0:GP, 10 * HE:10 * HE + HALVES]
        highest = flat_a[0:GP, 10 * HE + 2:10 * HE + 2 + HALVES]
        extra = flat_a[0:GP, 10 * HE + 4:10 * HE + 4 + HALVES]
        msg_b = [flat_h[:, at:at + NODE_TILES * RELS * P].rearrange("p (j e) -> p j e", j=NODE_TILES)
                 for flat_h in (h_b[:].rearrange("p a k n -> p (a k n)"),) for at in (2 * N, 9 * N)]
        msgs_a = (msg[:, :, 0, :], msg[:, :, 1, :])
        early_msgs, early_accs = (msgs_a, msg_b), (acc, acc_b)
        stats = part[:, P:P + 120].rearrange("p (j s) -> p j s", j=NODE_TILES)
        mean_var = part[:, 250:270].rearrange("p (j s) -> p j s", j=NODE_TILES)
        var_eps, std, rstd, newton, newton2 = (part[:, 270 + 10 * k:280 + 10 * k] for k in range(5))
        emb = part[0:RELS, 0:TYPE_DIM]
        bias_rows = w_raw[0:BLOCKS, 0:P]
        iota_i = w_raw[:, P:P + WIN_COLS].bitcast(I32)
        part_id_i = w_raw[:, 600:601].bitcast(I32)
        part_id = w_raw[:, 602:603]
        row_f = w_raw[0:1, 640:640 + 2 * GROUPS].rearrange("p (a g) -> p a g", a=2)
        most_f = w_raw[0:1, 1000:1001]
        hot_type = acc_b[0:RELS, :]
        type_i = acc[0:RELS, :].bitcast(I32)
        scan_bufs = (flat_mf[:, 0:MATS * T[0] * P], flat_w[:, 0:MATS * T[0] * P])
        flat_ih = flat_i.bitcast(F16)
        ring_main = flat_ih[:, 0:RING * SUBS * WIN_COLS].rearrange("p (s u c) -> p s u c", s=RING, u=SUBS)
        ring_src = flat_ih[:, RING * SUBS * WIN_COLS:RING * SUBS * (WIN_COLS + P)].rearrange(
            "p (s u c) -> p s u c", s=RING, u=SUBS)
        used = RING * SUBS * (WIN_COLS + P) // 2
        keys_t = flat_i[0:SUB, used:used + 4 * SUBS * GROUPS].rearrange("p (a u g) -> p a u g", a=4, u=SUBS)
        used += 4 * SUBS * GROUPS
        iota_h = flat_i[:, used:used + WIN_COLS // 2].bitcast(F16)
        used += WIN_COLS // 2
        row_i = flat_i[0:1, used:used + GROUPS].bitcast(I32)
        used += GROUPS
        most_i = flat_i[0:1, used:used + 1].bitcast(I32)
        far = flat_i[0:SUB, used + 2:used + 10]
        ring_keys = flat_i[0:SUB, used + 10:used + 10 + RING]
        gate = flat_i[0:SUB, used + 14:used + 15 + RING]
        shifts = flat_i[0:SUB, used + 20:used + 21]
        assert used + 21 <= RELS * N
        resid = flat_b[:, 0:2 * NODE_TILES * P].rearrange("p (s j c) -> p s j c", s=2, j=NODE_TILES)

        pair = ctx.enter_context(nc.psum_tensor("pair", [P, 2, BANK], F32))
        trio = ctx.enter_context(nc.psum_tensor("trio", [P, 2, 3, BANK], F32))

        edges_in, x_in, small_in = sem("edges_in"), sem("x_in"), sem("small_in")
        consts_made, counts_zeroed = sem("consts_made"), sem("counts_zeroed")
        keys_made, keys_turned, keys_kept = sem("keys_made"), sem("keys_turned"), sem("keys_kept")
        rows_made, rows_kept = sem("rows_made"), sem("rows_kept")
        main_hot, src_hot, ring_keyed = sem("main_hot"), sem("src_hot"), sem("ring_keyed")
        group_counted, group_added = sem("group_counted"), sem("group_added")
        far_hot, far_counted, far_added = sem("far_hot"), sem("far_counted"), sem("far_added")
        counts_done = sem("counts_done")
        degrees_ready, degrees_taken = sem("degrees_ready"), sem("degrees_taken")
        var_ready, std_ready, x_normed = sem("var_ready"), sem("std_ready"), sem("x_normed")
        h0_ready, h0_hi, h0_lo = sem("h0_ready"), sem("h0_hi"), sem("h0_lo")
        scan_in, scan_used = (sem("scan_in_a"), sem("scan_in_b")), sem("scan_used")
        w_in, w_hi, w_used = sem("w_in"), sem("w_hi"), sem("w_used")
        max_local, max_over_all, scales_ready = sem("max_local"), sem("max_over_all"), sem("scales_ready")
        msg_ready, msg_hi, msg_split = sem("msg_ready"), sem("msg_hi"), sem("msg_split")
        root_ready, root_taken = sem("root_ready"), sem("root_taken")
        rel_ready, rel_taken, rel_added = sem("rel_ready"), sem("rel_taken"), sem("rel_added")
        h_scaled, h_hi, block_done = sem("h_scaled"), sem("h_hi"), sem("block_done")
        resid_in, out_turned, out_added, stored = sem("resid_in"), sem("out_turned"), sem("out_added"), sem("stored")
        bias_turned = sem("bias_turned")
        dve_step, far_step = sem("dve_step"), sem("far_step")

        def own_view(l, half):
            ks = 4 if half == 0 else K_TILES[l] - 4
            return ks, w_raw[:, 0:ks * MATS * P]

        block = ctx.enter_context(nc.Block())

        @block.sync
        def _(sp):
            for a, arr in enumerate((dst, src, edge_type)):
                sp.dma_start(ed[:, a], arr.rearrange("(h p i) -> p h i", h=HALVES, p=GP)
                             ).then_inc(edges_in, 16)
            for r in range(RELS):
                sp.dma_start(type_i[r:r + 1, :], node_type.rearrange("(a n) -> a n", a=1)
                             ).then_inc(small_in, 16)
            sp.dma_start(emb, node_emb).then_inc(small_in, 16)
            for l in range(LAYERS):
                sp.dma_start(bias_rows[FIRST[l]:FIRST[l] + T[l], :],
                             bias[l].rearrange("(t p) -> t p", p=P)).then_inc(small_in, 16)
            sp.dma_start(x_sb[:, 0:NODE_TILES - 1, :],
                         x[0:FULL_ROWS, :].rearrange("(j p) c -> p j c", p=P)).then_inc(x_in, 16)
            sp.dma_start(x_sb[0:LAST_ROWS, NODE_TILES - 1, :], x[FULL_ROWS:N, :]).then_inc(x_in, 16)

            def load_scan(l, kt, half):
                cols = T[l] * P
                for q in range(2):
                    sp.dma_start(w_raw[:, q * cols:(q + 1) * cols],
                                 mats[l][2 * half + q][bass.ds(kt * P, P), :]).then_inc(w_in, 16)

            def load_own(l, t, half):
                ks, raw = own_view(l, half)
                view = raw.rearrange("p (k m e) -> p k m e", k=ks, m=MATS)
                for m in range(MATS):
                    rows = mats[l][m][half * 4 * P:(half * 4 + ks) * P, bass.ds(t * P, P)]
                    sp.dma_start(view[:, :, m, :], rows.rearrange("(k p) e -> p k e", p=P)
                                 ).then_inc(w_in, 16)

            for n in range(SCANS0):
                if n >= 2:
                    sp.wait_ge(scan_used, n - 1)
                for m in range(MATS):
                    sp.dma_start(scan_bufs[n % 2][:, m * T[0] * P:(m + 1) * T[0] * P],
                                 mats[0][m][n * P:(n + 1) * P, :]).then_inc(scan_in[n % 2], 16)
            sp.wait_ge(rows_kept, 1)
            load_own(0, 0, 0)
            sp.wait_ge(w_used, 1)
            load_own(0, 0, 1)

            def block_loads(l, t, next_l, next_t):
                before = used_before(l, t)
                for half in range(scans(l)):
                    sp.wait_ge(w_used, before + half)
                    load_scan(l + 1, t, half)
                if l == LAST:
                    slot = sp.snap(t % 2)
                    sp.wait_ge(stored, 32 * t + STORE_CREDIT - 32)
                    sp.wait_ge(resid_in, 32 * t + RESID_CREDIT)
                    for j0, nj, rows in ((0, NODE_TILES - 1, P), (NODE_TILES - 1, 1, LAST_ROWS)):
                        sp.dma_start(
                            resid[0:rows, bass.ds(slot, 1), j0:j0 + nj, :].rearrange("p s j c -> p (s j) c"),
                            x[j0 * P:j0 * P + nj * rows, bass.ds(t * P, P)].rearrange("(j p) c -> p j c", p=rows)
                        ).then_inc(resid_in, 16)
                if next_l is not None:
                    for half in range(2):
                        sp.wait_ge(w_used, before + scans(l) + half)
                        load_own(next_l, next_t, half)

            for l in range(LAYERS):
                if l == LAST:
                    sp.wait_ge(root_ready, FIRST[LAST])
                with sp.Fori(0, T[l] - 1) as t:
                    block_loads(l, t, l, t + 1)
                block_loads(l, T[l] - 1, l + 1 if l < LAST else None, 0)

        @block.gpsimd
        def _(pool):
            pool.iota(iota_i, [[1, WIN_COLS]], base=0, channel_multiplier=0).then_inc(consts_made, 1)
            pool.iota(part_id_i, [[0, 1]], base=0, channel_multiplier=1).then_inc(consts_made, 1)
            pool.memset(ident[:], 1.0).then_inc(consts_made, 1)
            pool.wait_ge(consts_made, 3)
            pool.affine_select(out=ident[:], in_=ident[:], compare_op=ALU.is_equal, fill=0.0, base=0,
                               pattern=[[-1, P]], channel_multiplier=1).then_inc(consts_made, 1)
            pool.memset(ones_h[:], 1.0).then_inc(consts_made, 1)
            pool.memset(counts[:, NODE_TILES // 2:], 0.0).then_inc(counts_zeroed, 1)

            def join(n):
                pool.wait_ge(max_local, n)
                pool.partition_all_reduce(over_all[:], local[:], P, RMAX).then_inc(max_over_all, 1)

            join(1)
            join(2)
            pool.wait_ge(keys_kept, 2)
            with pool.Fori(0, GROUPS // RING) as it:
                pool.wait_ge(src_hot, it * RING + SRC_CREDIT)
                pool.tensor_copy(ring_keys, keys_t[:, 1, 0, bass.ds(it * RING, RING)]).then_inc(ring_keyed, 1)
                pool.wait_ge(ring_keyed, it + 1)
                pool.tensor_tensor(gate[:, RING:RING + 1], ident[0:SUB, 0:1], ident[0:SUB, 0:1], ALU.mult)
                for slot in range(RING):
                    g = it * RING + slot
                    pool.wait_ge(group_counted, g + RING_CREDIT - RING + 1)
                    pool.tensor_tensor(gate[:, slot:slot + 1], ident[0:SUB, 0:1], ident[0:SUB, 0:1], ALU.mult)
                    pool.tensor_scalar(ring_src[0:SUB, slot, 0, :], iota_h[0:SUB, 0:P],
                                       ring_keys[:, slot:slot + 1], None, ALU.is_equal).then_inc(src_hot, 1)
            for n in range(3, 7):
                join(n)

        @block.scalar
        def _(act):
            act.wait_ge(var_ready, 1)
            nc.scalar.activation(std, var_eps, ACT.Sqrt).then_inc(std_ready, 1)
            for k in range(K_TILES[0]):
                act.wait_ge(h0_ready, k + 1)
                for c, (c0, cw) in enumerate(H0_CHUNKS):
                    last = nc.scalar.activation(h_a[:, 0, k, c0:c0 + cw], trio[:, k % 2, c, 0:cw],
                                                ACT.Relu if k < IN_CH // P else ACT.Copy)
                last.then_inc(h0_hi, 1)

            def split_w(l, t, half, in_count):
                ks, raw = own_view(l, half)
                act.wait_ge(w_in, in_count)
                nc.scalar.activation(
                    w_split[:, 4 * half:4 * half + ks, 0].rearrange("p k m e -> p k (m e)"),
                    raw.rearrange("p (k e) -> p k e", k=ks), ACT.Copy, scale=sc[:, l, W_SCALE:W_SCALE + 1]
                ).then_inc(w_hi, 1)

            act.wait_ge(scales_ready, w_scaled_at(0))
            split_w(0, 0, 0, OWN_INC)
            split_w(0, 0, 1, IN0)

            def store(t):
                act.wait_ge(out_added, t + 1)
                act.wait_ge(stored, 32 * t + STORE_CREDIT)
                slot = act.snap(t % 2)
                for j0, nj, rows in ((0, NODE_TILES - 1, P), (NODE_TILES - 1, 1, LAST_ROWS)):
                    act.dma_start(
                        out[j0 * P:j0 * P + nj * rows, bass.ds(t * P, P)].rearrange("(j p) c -> p j c", p=rows),
                        resid[0:rows, bass.ds(slot, 1), j0:j0 + nj, :].rearrange("p s j c -> p (s j) c")
                    ).then_inc(stored, 16)

            def high_messages(l, g, msgs):
                for j in range(NODE_TILES):
                    rows = P if j < NODE_TILES - 1 else LAST_ROWS
                    act.wait_ge(msg_ready, NODE_TILES * g + j + 1)
                    nc.scalar.activation(msgs[0][0:rows, j, :], pair[0:rows, j % 2, 0:RELS * P], ACT.Copy,
                                         scale=sc[0:rows, l, M_SCALE:M_SCALE + 1]).then_inc(msg_hi, 1)

            def take_root(l, g, to):
                act.wait_ge(root_ready, g + 1)
                for c, (c0, cw) in enumerate(CHUNKS):
                    last = nc.scalar.activation(to[:, c0:c0 + cw], trio[:, 0, c, 0:cw], ACT.Identity,
                                                bias=bias_sb[:, bass.ds(g, 1)],
                                                scale=sc[:, l, ROOT_BACK:ROOT_BACK + 1])
                last.then_inc(root_taken, 1)

            def split_next(l, t, next_l, next_t):
                act.wait_ge(scales_ready, w_scaled_at(next_l))
                for half in range(2):
                    split_w(next_l, next_t, half, in_before(l, t) + scans(l) * SCAN_INC + (half + 1) * OWN_INC)

            def high_h(l, t, done):
                act.wait_ge(h_scaled, FIRST[l] + t + 1)
                nc.scalar.activation(h_in[l + 1][:, 0, bass.ds(t, 1), :].rearrange("p k n -> p (k n)"),
                                     done[:], ACT.Copy).then_inc(h_hi, 1)

            def act_block(l, t, next_l, next_t, stores):
                g = FIRST[l] + t
                high_messages(l, g, msgs_a)
                if stores:
                    store(t - 1)
                if l < LAST:
                    act.wait_ge(block_done, g + DONE_CREDIT)
                take_root(l, g, acc)
                if next_l is not None:
                    split_next(l, t, next_l, next_t)
                if l < LAST:
                    high_h(l, t, acc)

            for l in range(LAYERS):
                act.wait_ge(scales_ready, m_scaled_at(l))
                if l == 0:
                    for b in range(EARLY):
                        high_messages(0, b, early_msgs[b])
                        take_root(0, b, early_accs[b])
                        split_next(0, b, 0, b + 1)
                    for b in range(EARLY):
                        high_h(0, b, early_accs[b])
                if l == LAST:
                    act.wait_ge(block_done, FIRST[LAST] + DONE_CREDIT)
                    act_block(l, 0, l, 1, False)
                with act.Fori(START[l], T[l] - 1) as t:
                    act_block(l, t, l, t + 1, l == LAST)
                act_block(l, T[l] - 1, l + 1 if l < LAST else None, 0, l == LAST)
            store(T[LAST] - 1)
            act.wait_ge(stored, 32 * T[LAST] + STORE_CREDIT)

        @block.vector
        def _(dve):
            steps = Steps(dve, dve_step)
            then = steps.then
            V = nc.vector

            V.memset(counts[:, 0:NODE_TILES // 2], 0.0).then_inc(counts_zeroed, 1)

            dve.wait_ge(edges_in, 48)
            d_i = ed[:, 0]
            src_f = ed[:, 1].rearrange("p h i -> p (h i)")
            rel_f = ed[:, 2].rearrange("p h i -> p (h i)")
            flat = [keys[:, a].rearrange("p h u i -> p (h u i)") for a in range(4)]
            V.tensor_scalar(src_hi, src_f, 7, None, ALU.logical_shift_right)
            V.tensor_scalar(src_lo, src_f, P - 1, None, ALU.bitwise_and)
            V.tensor_reduce(highest, d_i, AX.X, ALU.max)
            then(V.tensor_reduce(lowest, d_i, AX.X, ALU.min))
            for h in range(HALVES):
                V.tensor_scalar(keys[:, 3, h].rearrange("p u i -> p (u i)"), d_i[:, h, :], lowest[:, h:h + 1],
                                None, ALU.subtract)
            V.tensor_copy(flat[1], src_lo)
            V.tensor_tensor(extra, highest, lowest, ALU.subtract)
            then(V.tensor_scalar(key_tmp, rel_f, float(WIN), 1.0, ALU.mult, ALU.add))
            then(V.scalar_tensor_tensor(out=flat[2], in0=src_hi, scalar=float(RELS * WIN), in1=key_tmp,
                                        op0=ALU.mult, op1=ALU.add))
            then(V.tensor_scalar(extra, extra, 0.5, 1.0 / WIN, ALU.add, ALU.mult))
            then(V.tensor_scalar(extra, extra, -0.5, None, ALU.add))
            then(V.tensor_tensor(key_tmp, flat[2], flat[3], ALU.add))
            then(V.scalar_tensor_tensor(out=key_tmp, in0=flat[3], scalar=float(WIN), in1=key_tmp,
                                        op0=ALU.is_lt, op1=ALU.mult))
            V.tensor_scalar(flat[0], key_tmp, -1.0, None, ALU.add).then_inc(keys_made, 1)

            dve.wait_ge(small_in, 16 * (RELS + 1 + LAYERS))
            dve.wait_ge(consts_made, 5)
            dve.wait_ge(bias_turned, 1)
            then(V.tensor_copy(bias_sb[:], pair[:, 1, 0:BLOCKS]))
            V.tensor_copy(iota_h, iota_i)
            V.tensor_copy(part_id, part_id_i)
            then(V.memset(local[:], 0.0))
            V.tensor_reduce(local[0:RELS, 0:1], emb, AX.X, ALU.max, apply_absolute_value=True)
            V.tensor_reduce(local[:, 1:2], bias_sb[:], AX.X, ALU.max,
                            apply_absolute_value=True).then_inc(max_local, 1)

            def c_(l, k):
                return sc[:, l, k:k + 1]

            def scale_of(l, bound, scale, back):
                then(V.tensor_scalar(c_(l, back).bitcast(I32), c_(l, bound).bitcast(I32), EXPONENT, None,
                                     ALU.bitwise_and))
                then(V.tensor_scalar(c_(l, scale).bitcast(I32), c_(l, back).bitcast(I32), -1.0, INVERSE_BITS,
                                     ALU.mult, ALU.add))
                V.tensor_scalar(c_(l, scale), c_(l, scale), TOP, None, ALU.mult)
                return V.tensor_scalar(c_(l, back), c_(l, back), 1.0 / TOP, None, ALU.mult)

            dve.wait_ge(max_over_all, 1)
            V.tensor_copy(bias_max[:], over_all[:, 1:2])
            then(V.tensor_scalar(c_(0, B1), over_all[:, 0:1], LN_BOUND, None, ALU.max))
            then(scale_of(0, B1, H_SCALE, H_BACK))
            then(V.tensor_tensor(c_(0, H_TOP), c_(0, B1), c_(0, H_SCALE), ALU.mult))
            V.tensor_copy(local[:, 0:1], c_(0, H_TOP)).then_inc(scales_ready, 1)
            V.tensor_scalar(hot_type, type_i, part_id[0:RELS], c_(0, H_SCALE)[0:RELS],
                            ALU.is_equal, ALU.mult).then_inc(x_normed, 1)

            def scan_first(n):
                dve.wait_ge(scan_in[n % 2], (n // 2 + 1) * MATS * 16)
                V.tensor_reduce(tile_max[:, n:n + 1], scan_bufs[n % 2], AX.X, ALU.max,
                                apply_absolute_value=True).then_inc(scan_used, 1)

            dve.wait_ge(x_in, 32)
            for j in range(NODE_TILES):
                rows = P if j < NODE_TILES - 1 else LAST_ROWS
                for s in range(2):
                    V.bn_stats(stats[0:rows, j, 6 * s:6 * s + 6], x_sb[0:rows, j, 384 * s:384 * s + 384])
            if LAST_ROWS < P:
                V.memset(mean_var[:, NODE_TILES - 1, :], 1.0)
            then(V.tensor_copy(local[:, 1:2], bias_max[:]))
            for j in range(NODE_TILES):
                rows = P if j < NODE_TILES - 1 else LAST_ROWS
                ins = V.bn_aggr(mean_var[0:rows, j, :], stats[0:rows, j, :])
            then(ins)
            V.tensor_scalar(var_eps, mean_var[:, :, 1], EPS, None, ALU.add).then_inc(var_ready, 1)
            dve.wait_ge(std_ready, 1)
            then(V.reciprocal(rstd, std))
            then(V.tensor_tensor(newton, rstd, rstd, ALU.mult))
            then(V.tensor_tensor(newton2, newton, var_eps, ALU.mult))
            then(V.tensor_scalar(newton, newton2, -0.5, 1.5, ALU.mult, ALU.add))
            then(V.tensor_tensor(newton2, newton, rstd, ALU.mult))
            then(V.tensor_scalar(rstd, newton2, c_(0, H_SCALE), None, ALU.mult))
            for j in range(NODE_TILES):
                rows = P if j < NODE_TILES - 1 else LAST_ROWS
                ins = V.tensor_scalar(x_sb[0:rows, j, :], x_sb[0:rows, j, :], mean_var[0:rows, j, 0:1],
                                      rstd[0:rows, j:j + 1], ALU.subtract, ALU.mult)
            ins.then_inc(x_normed, 1)

            scan_first(0)
            scan_first(1)
            for a in range(4):
                dve.wait_ge(keys_turned, a + 1)
                V.tensor_copy(keys_t[:, a], trio[0:SUB, a % 2, a // 2, 0:SUBS * GROUPS].rearrange(
                    "p (u g) -> p u g", u=SUBS)).then_inc(keys_kept, 1)
            dve.wait_ge(rows_made, 1)
            then(V.tensor_copy(row_f, pair[0:1, 0, 0:2 * GROUPS].rearrange("p (a g) -> p a g", a=2)))
            V.tensor_copy(row_i, row_f[:, 0, :])
            then(V.tensor_reduce(most_f, row_f[:, 1, :], AX.X, ALU.max))
            V.tensor_copy(most_i, most_f).then_inc(rows_kept, 1)

            for k in range(K_TILES[0]):
                dve.wait_ge(h0_hi, k + 1)
                for c, (c0, cw) in enumerate(H0_CHUNKS):
                    if k < IN_CH // P:
                        ins = V.scalar_tensor_tensor(out=h_a[:, 1, k, c0:c0 + cw], in0=trio[:, k % 2, c, 0:cw],
                                                     scalar=0.0, in1=h_a[:, 0, k, c0:c0 + cw],
                                                     op0=ALU.max, op1=ALU.subtract)
                    else:
                        ins = V.tensor_tensor(h_a[:, 1, k, c0:c0 + cw], trio[:, k % 2, c, 0:cw],
                                              h_a[:, 0, k, c0:c0 + cw], ALU.subtract)
                ins.then_inc(h0_lo, 1)
                if k + 2 < SCANS0:
                    scan_first(k + 2)

            def hot_rows(g, slot):
                dve.wait_ge(group_counted, g + RING_CREDIT - RING + 1)
                for u in range(SUBS):
                    ins = V.tensor_scalar(ring_main[0:SUB, slot, u, :], iota_h[0:SUB, :],
                                          keys_t[:, 0, u, bass.ds(g, 1)], None, ALU.is_equal)
                for u in range(1, SUBS):
                    ins = V.tensor_scalar(ring_src[0:SUB, slot, u, :], iota_h[0:SUB, 0:P],
                                          keys_t[:, 1, u, bass.ds(g, 1)], None, ALU.is_equal)
                ins.then_inc(main_hot, 1)

            def add_window(bank, first):
                view = counts[:, :, :, bass.ds(first, WIN)]
                return V.tensor_tensor(view, view, trio[:, 1, bank, 0:WIN_COLS].rearrange(
                    "p (j r d) -> p j r d", j=NODE_TILES, r=RELS), ALU.add)

            def first_of(g, groups=1):
                return nc.values_load_multi_w_load_instructions(
                    row_i[0:1, bass.ds(g, groups)], engines=(mybir.EngineType.DVE,), min_val=0, max_val=N - 1,
                    skip_runtime_bounds_check_because="minima of dst, whose values number the N nodes")[1]

            def add_group(g, bank, first):
                dve.wait_ge(group_counted, g + RING_CREDIT + 1)
                dve.wait_ge(group_added, g + BANK_CREDIT)
                add_window(bank, first).then_inc(group_added, 1)

            def scan(in_count, cols, at):
                dve.wait_ge(w_in, in_count)
                V.tensor_reduce(tile_max[:, at:at + 1] if isinstance(at, int) else tile_max[:, bass.ds(at, 1)],
                                w_raw[:, 0:2 * cols], AX.X, ALU.max,
                                apply_absolute_value=True).then_inc(w_used, 1)

            def joined(n, column, maxima):
                V.tensor_reduce(local[:, column:column + 1], maxima, AX.X, ALU.max).then_inc(max_local, 1)
                dve.wait_ge(max_over_all, n)

            def weight_scales(l, n):
                if l:
                    dve.wait_ge(w_used, used_before(l - 1, T[l - 1] - 1) + 2)
                else:
                    dve.wait_ge(scan_used, SCANS0)
                joined(n, 0, tile_max[:, 0:SCANS0 if l == 0 else 2 * K_TILES[l]])
                then(V.tensor_scalar(c_(l, W_MAX), over_all[:, 0:1], TINY, None, ALU.max))
                scale_of(l, W_MAX, W_SCALE, W_BACK).then_inc(scales_ready, 1)

            def message_scales(l):
                dve.wait_ge(scales_ready, w_scaled_at(l))
                then(V.tensor_tensor(c_(l, B1), c_(l, W_MAX), c_(l, W_SCALE), ALU.mult))
                then(V.tensor_tensor(c_(l, B1), c_(l, B1), c_(l, H_TOP), ALU.mult))
                then(V.tensor_scalar(c_(l, B1), c_(l, B1), K_BOUND, TINY, ALU.mult, ALU.max))
                then(scale_of(l, B1, M_SCALE, M_BACK))
                then(V.tensor_tensor(c_(l, ROOT_BACK), c_(l, H_BACK), c_(l, W_BACK), ALU.mult))
                ins = V.tensor_tensor(c_(l, REL_BACK), c_(l, ROOT_BACK), c_(l, M_BACK), ALU.mult)
                if l < LAST:
                    then(ins)
                    then(V.tensor_tensor(c_(l + 1, B2), c_(l, H_TOP), c_(l, H_BACK), ALU.mult))
                    then(V.tensor_tensor(c_(l + 1, B2), c_(l + 1, B2), c_(l, W_MAX), ALU.mult))
                    then(V.tensor_scalar(c_(l + 1, B2), c_(l + 1, B2), MATS * K_BOUND, bias_max[:],
                                         ALU.mult, ALU.add))
                    then(V.tensor_scalar(c_(l + 1, B2), c_(l + 1, B2), TINY, None, ALU.max))
                    ins = scale_of(l + 1, B2, H_SCALE, H_BACK)
                ins.then_inc(scales_ready, 1)
                dve.wait_ge(scales_ready, m_scaled_at(l))

            def low_w(l, half, nth_hi):
                ks, raw = own_view(l, half)
                dve.wait_ge(w_hi, nth_hi)
                to = w_split[:, 4 * half:4 * half + ks]
                V.scalar_tensor_tensor(out=to[:, :, 1].rearrange("p k m e -> p k (m e)"),
                                       in0=raw.rearrange("p (k e) -> p k e", k=ks), scalar=c_(l, W_SCALE),
                                       in1=to[:, :, 0].rearrange("p k m e -> p k (m e)"),
                                       op0=ALU.mult, op1=ALU.subtract).then_inc(w_used, 1)

            def low_message(l, g, j, bank, rows, msgs):
                dve.wait_ge(msg_hi, NODE_TILES * g + j + 1)
                hi, lo = (m[0:rows, bass.ds(j, 1), :].rearrange("p j e -> p (j e)") for m in msgs)
                V.scalar_tensor_tensor(out=lo, in0=pair[0:rows, bank, 0:RELS * P],
                                       scalar=c_(l, M_SCALE)[0:rows], in1=hi,
                                       op0=ALU.mult, op1=ALU.subtract).then_inc(msg_split, 1)

            def scan_next(l, t, half):
                scan(in_before(l, t) + (half + 1) * SCAN_INC, T[l + 1] * P, 2 * t + half)

            def count_round(it):
                firsts = first_of(it * RING, RING)
                for slot in range(RING):
                    g = it * RING + slot
                    add_group(g, slot % 2, firsts[slot])
                    hot_rows(g + RING, slot)

            weight_scales(0, 2)
            message_scales(0)
            dve.wait_ge(counts_zeroed, 2)
            dve.wait_ge(rows_kept, 1)
            for slot in range(RING):
                hot_rows(slot, slot)
            for n in range(ROUNDS_FIRST):
                count_round(n)
                if n < 2:
                    low_w(0, n, n + 1)

            for b in range(EARLY):
                base = ROUNDS_FIRST + b * EARLY_ROUNDS
                for half in range(2):
                    with dve.Fori(2 * half, 2 * half + 2) as jj:
                        for bank in range(2):
                            count_round(base + 2 * jj + bank)
                            low_message(0, b, 2 * jj + bank, bank, P, early_msgs[b])
                    scan_next(0, b, half)
                for j in range(NODE_TILES - 2, NODE_TILES):
                    count_round(base + j)
                    low_message(0, b, j, j % 2, P if j < NODE_TILES - 1 else LAST_ROWS, early_msgs[b])
                with dve.Fori(base + NODE_TILES, base + NODE_TILES + K_TILES[0]) as it:
                    count_round(it)
                if b < EARLY - 1:
                    for half in range(ROUNDS_SPLIT):
                        count_round(base + NODE_TILES + K_TILES[0] + half)
                        low_w(0, half, 2 * b + 2 + half + 1)
            firsts = first_of(GROUPS - RING, RING)
            for slot in range(RING):
                add_group(GROUPS - RING + slot, slot % 2, firsts[slot])

            most = dve.value_load(most_i, min_val=0, max_val=N // WIN)
            with dve.If(most > 0):
                dve.wait_ge(group_added, GROUPS + BANK_CREDIT)
                far_steps = Steps(dve, far_step)
                with dve.Fori(0, GROUPS) as g:
                    first = first_of(g)[0]
                    with dve.Fori(1, most + 1) as s:
                        v = dve.snap(g * most + s)
                        start = dve.snap((first + s * WIN) % (LAST_WIN + 1))
                        shift, rel, inside, key = far[:, 0:1], far[:, 1:3], far[:, 3:5], far[:, 5:7]
                        far_steps.base, far_steps.count = (v - 1) * FAR_STEPS, 0
                        fthen = far_steps.then
                        fthen(V.tensor_scalar(shift, iota_h[0:SUB, bass.ds(s, 1)], float(WIN), None, ALU.mult))
                        fthen(V.tensor_scalar(rel, keys_t[:, 3, :, bass.ds(g, 1)].rearrange("p u g -> p (u g)"),
                                              shift, None, ALU.subtract))
                        fthen(V.tensor_scalar(inside, rel, 0.0, None, ALU.is_ge))
                        fthen(V.tensor_tensor(key, keys_t[:, 2, :, bass.ds(g, 1)].rearrange("p u g -> p (u g)"),
                                              rel, ALU.add))
                        fthen(V.tensor_tensor(key, key, inside, ALU.mult))
                        fthen(V.scalar_tensor_tensor(out=key, in0=rel, scalar=float(WIN), in1=key,
                                                     op0=ALU.is_lt, op1=ALU.mult))
                        fthen(V.tensor_scalar(key, key, -1.0, None, ALU.add))
                        for u in range(SUBS):
                            V.tensor_scalar(ring_main[0:SUB, 0, u, :], iota_h[0:SUB, :], key[:, u:u + 1],
                                            None, ALU.is_equal)
                            ins = V.tensor_scalar(ring_src[0:SUB, 0, u, :], iota_h[0:SUB, 0:P],
                                                  keys_t[:, 1, u, bass.ds(g, 1)], None, ALU.is_equal)
                        ins.then_inc(far_hot, 1)
                        dve.wait_ge(far_counted, v)
                        add_window(0, start).then_inc(far_added, 1)
                        dve.wait_ge(far_added, v)

            dve.wait_ge(group_added, GROUPS + BANK_CREDIT)
            V.memset(local[:, 1:2], 0.0).then_inc(counts_done, 1)

            for r in range(RELS):
                dve.wait_ge(degrees_ready, r + 1)
                for c, (c0, cw) in enumerate(CHUNKS):
                    ins = V.tensor_scalar(inv[:, r, c0:c0 + cw], trio[:, r % 2, c, 0:cw], 1.0, None, ALU.max)
                ins.then_inc(degrees_taken, 1)
            dve.wait_ge(degrees_taken, RELS)

            def add_relation(l, g, r, to):
                dve.wait_ge(rel_ready, RELS * g + r + 1)
                for c, (c0, cw) in enumerate(CHUNKS):
                    nth = 9 * g + 3 * r + c
                    V.scalar_tensor_tensor(out=part[:, 0:cw], in0=trio[:, (r + 1) % 2, c, 0:cw],
                                           scalar=c_(l, REL_BACK), in1=inv[:, r, c0:c0 + cw],
                                           op0=ALU.mult, op1=ALU.mult).then_inc(rel_taken, 1)
                    dve.wait_ge(rel_taken, nth + 1 + SLOT_CREDIT)
                    if r == 0 and c == 0:
                        dve.wait_ge(root_taken, g + 1)
                    V.tensor_tensor(to[:, c0:c0 + cw], to[:, c0:c0 + cw], part[:, 0:cw],
                                    ALU.add).then_inc(rel_added, 1)
                    dve.wait_ge(rel_added, nth + 1)

            def add_residual(t):
                dve.wait_ge(out_turned, t + 1)
                dve.wait_ge(resid_in, 32 * (t + 1) + RESID_CREDIT)
                slot = dve.snap(t % 2)
                for bank, (j0, nj, rows) in enumerate(((0, 4, P), (4, 4, P), (8, 1, P), (9, 1, LAST_ROWS))):
                    view = resid[0:rows, bass.ds(slot, 1), j0:j0 + nj, :].rearrange("p s j c -> p (s j c)")
                    at = (j0 % 4) * P
                    ins = V.tensor_tensor(view, view, trio[0:rows, 0, j0 // 4, at:at + nj * P], ALU.add)
                ins.then_inc(out_added, 1)

            def add_block(l, t, to, next_l, nth_hi):
                g = FIRST[l] + t
                for r in range(RELS):
                    if next_l is not None and r < 2:
                        low_w(next_l, r, nth_hi + r + 1)
                    if l == 0 and isinstance(t, int) and t == 0:
                        then(V.reciprocal(inv[:, r, :], inv[:, r, :]))
                    add_relation(l, g, r, to)
                if l == LAST:
                    V.tensor_scalar(to[:], to[:], 0.0, None, ALU.max).then_inc(h_scaled, 1)
                    return
                V.tensor_scalar(to[:], to[:], 0.0, c_(l + 1, H_SCALE), ALU.max,
                                ALU.mult).then_inc(h_scaled, 1)
                dve.wait_ge(h_scaled, g + 1)
                V.tensor_reduce(tile_max[:, bass.ds(2 * T[0] + t, 1)], to[:], AX.X, ALU.max)
                dve.wait_ge(h_hi, g + 1)
                h_next = h_in[l + 1]
                V.tensor_tensor(h_next[:, 1, bass.ds(t, 1), :].rearrange("p k n -> p (k n)"), to[:],
                                h_next[:, 0, bass.ds(t, 1), :].rearrange("p k n -> p (k n)"),
                                ALU.subtract).then_inc(block_done, 1)

            def dve_block(l, t, next_l, adds):
                g = FIRST[l] + t
                for j in range(NODE_TILES):
                    low_message(l, g, j, j % 2, P if j < NODE_TILES - 1 else LAST_ROWS, msgs_a)
                    if l < LAST and j in (3, 7):
                        scan_next(l, t, j // 4)
                if l < LAST and next_l == l + 1:
                    weight_scales(l + 1, 3 + 2 * l)
                if adds:
                    add_residual(t - 1)
                add_block(l, t, acc, next_l, 2 * g + 2)

            for b in range(EARLY):
                add_block(0, b, early_accs[b], 0 if b == 0 else None, 2 * EARLY)
            for l in range(LAYERS):
                if l:
                    dve.wait_ge(block_done, FIRST[l] + DONE_CREDIT)
                    joined(2 + 2 * l, 1, tile_max[:, 2 * T[0]:2 * T[0] + T[l - 1]])
                    then(V.tensor_copy(c_(l, H_TOP), over_all[:, 1:2]))
                    message_scales(l)
                if l == LAST:
                    dve_block(l, 0, l, False)
                with dve.Fori(START[l], T[l] - 1) as t:
                    dve_block(l, t, l, l == LAST)
                dve_block(l, T[l] - 1, l + 1 if l < LAST else None, l == LAST)
            add_residual(T[LAST] - 1)

        @block.tensor
        def _(pe):
            M = nc.tensor
            pe.sem_inc(group_counted, RING_CREDIT)
            pe.sem_inc(group_added, BANK_CREDIT)
            pe.sem_inc(msg_split, BANK_CREDIT)
            pe.sem_inc(rel_taken, SLOT_CREDIT)
            pe.sem_inc(stored, STORE_CREDIT)
            pe.sem_inc(resid_in, RESID_CREDIT)
            pe.sem_inc(block_done, DONE_CREDIT)
            pe.sem_inc(src_hot, SRC_CREDIT)

            pe.wait_ge(consts_made, 5)
            pe.wait_ge(small_in, 16 * (RELS + 1 + LAYERS))
            M.transpose(pair[:, 1, 0:BLOCKS], bias_rows, ident[0:BLOCKS, 0:BLOCKS]).then_inc(bias_turned, 1)
            pe.wait_ge(keys_made, 1)
            for a in range(4):
                for u in range(SUBS):
                    for h in range(HALVES):
                        at = u * GROUPS + h * GP
                        last = M.transpose(trio[0:SUB, a % 2, a // 2, at:at + GP], keys[:, a, h, u, :],
                                           ident[0:GP, 0:GP])
                last.then_inc(keys_turned, 1)
            for a, col in enumerate((lowest, extra)):
                for h in range(HALVES):
                    at = a * GROUPS + h * GP
                    last = M.matmul(pair[0:1, 0, at:at + GP], col[:, h:h + 1], ident[0:GP, 0:GP],
                                    start=True, stop=True, skip_group_check=True)
            last.then_inc(rows_made, 1)

            pe.wait_ge(keys_kept, 4)
            pe.wait_ge(x_normed, 2)
            for k in range(K_TILES[0]):
                if k >= 2:
                    pe.wait_ge(h0_lo, k - 1)
                if k < IN_CH // P:
                    for j in range(NODE_TILES):
                        rows = P if j < NODE_TILES - 1 else LAST_ROWS
                        at = (j % 4) * P
                        last = M.transpose(trio[:, k % 2, j // 4, at:at + rows],
                                           x_sb[0:rows, j, k * P:(k + 1) * P], ident[0:rows, 0:rows])
                else:
                    for c, (c0, cw) in enumerate(H0_CHUNKS):
                        last = M.matmul(trio[:, k % 2, c, 0:cw], emb, hot_type[:, c0:c0 + cw],
                                        start=True, stop=True)
                last.then_inc(h0_ready, 1)

            def count(slot, bank):
                for u in range(SUBS):
                    ins = M.matmul(trio[:, 1, bank, 0:WIN_COLS], ring_src[0:SUB, slot, u, :],
                                   ring_main[0:SUB, slot, u, :], start=(u == 0), stop=(u == SUBS - 1))
                return ins

            def count_round(it, beside=()):
                for slot in range(RING):
                    g = it * RING + slot
                    pe.wait_ge(main_hot, g + 1)
                    pe.wait_ge(src_hot, g + 1 + SRC_CREDIT)
                    pe.wait_ge(group_added, g + BANK_CREDIT - 1)
                    count(slot, slot % 2).then_inc(group_counted, 1)
                    if slot < len(beside):
                        beside[slot]()

            def messages(l, g, j, bank, rows, w_count, shares=1):
                passes = [(k, n, ph, pw) for k in range(K_TILES[l])
                          for n, (ph, pw) in enumerate(((0, 0), (0, 1), (1, 0)))]
                size = len(passes) // shares

                def share(s):
                    if s == 0:
                        pe.wait_ge(msg_split, NODE_TILES * g + j - 1 + BANK_CREDIT)
                        pe.wait_ge(w_used, w_count)
                    for k, n, ph, pw in passes[s * size:(s + 1) * size]:
                        last = M.matmul(pair[0:rows, bank, 0:RELS * P], h_in[l][:, ph, k, bass.ds(j * P, rows)],
                                        w_split[:, k, pw, 0:RELS, :].rearrange("p m e -> p (m e)"),
                                        start=(k == 0 and n == 0), stop=(k == K_TILES[l] - 1 and n == 2))
                    if s == shares - 1:
                        last.then_inc(msg_ready, 1)
                return [lambda s=s: share(s) for s in range(shares)]

            def root_pass(l, k, n, first, final):
                pw, ph = ((0, 0), (0, 1), (1, 0))[n]
                for c, (c0, cw) in enumerate(CHUNKS):
                    last = M.matmul(trio[:, 0, c, 0:cw],
                                    w_split[:, bass.ds(k, 1), pw, RELS, :].rearrange("p k e -> p (k e)"),
                                    h_in[l][:, ph, bass.ds(k, 1), c0:c0 + cw].rearrange("p k n -> p (k n)"),
                                    start=(first and n == 0), stop=(final and n == 2))
                return last

            def root(l):
                for k in range(K_TILES[l]):
                    for n in range(3):
                        last = root_pass(l, k, n, k == 0, k == K_TILES[l] - 1)
                return last

            def gather_tile(msgs, r, j, rows, start, stop):
                for pm in range(2):
                    for c, (c0, cw) in enumerate(CHUNKS):
                        last = M.matmul(trio[:, (r + 1) % 2, c, 0:cw],
                                        msgs[pm][0:rows, bass.ds(j, 1), r * P:(r + 1) * P].rearrange("p j e -> p (j e)"),
                                        counts[0:rows, bass.ds(j, 1), r, c0:c0 + cw].rearrange("p j n -> p (j n)"),
                                        start=start and pm == 0, stop=stop and pm == 1)
                return last

            def gathering(g, msgs):
                pe.wait_ge(msg_split, NODE_TILES * (g + 1) + BANK_CREDIT)
                for r in range(RELS):
                    if r == 1:
                        pe.wait_ge(root_taken, g + 1)
                    else:
                        pe.wait_ge(rel_taken, 9 * g + (3 if r == 2 else 0) + SLOT_CREDIT)
                    gather_tile(msgs, r, 0, P, True, False)
                    with pe.Fori(1, NODE_TILES - 1, 2) as j:
                        gather_tile(msgs, r, j, P, False, False)
                        gather_tile(msgs, r, j + 1, P, False, False)
                    gather_tile(msgs, r, NODE_TILES - 1, LAST_ROWS, False, True).then_inc(rel_ready, 1)

            def turn_out(t):
                pe.wait_ge(h_scaled, FIRST[LAST] + t + 1)
                pe.wait_ge(rel_taken, 9 * (FIRST[LAST] + t + 1) - 3 + SLOT_CREDIT)
                for j in range(NODE_TILES):
                    rows = P if j < NODE_TILES - 1 else LAST_ROWS
                    at = (j % 4) * P
                    last = M.transpose(trio[0:rows, 0, j // 4, at:at + P], acc[:, j * P:j * P + rows], ident[:])
                last.then_inc(out_turned, 1)

            def pe_block(l, t, turns):
                g = FIRST[l] + t
                w_count = used_before(l, t)
                with pe.Fori(0, NODE_TILES // 2 - 1) as jj:
                    for bank in range(2):
                        messages(l, g, 2 * jj + bank, bank, P, w_count)[0]()
                messages(l, g, NODE_TILES - 2, 0, P, w_count)[0]()
                messages(l, g, NODE_TILES - 1, 1, LAST_ROWS, w_count)[0]()
                if turns:
                    turn_out(t - 1)
                    pe.wait_ge(out_added, t)
                pe.wait_ge(rel_taken, 9 * g - 3 + SLOT_CREDIT)
                root(l).then_inc(root_ready, 1)
                gathering(g, msgs_a)

            pe.wait_ge(rows_kept, 1)
            pe.wait_ge(h0_lo, K_TILES[0])
            with pe.Fori(0, ROUNDS_FIRST) as it:
                count_round(it)
            for b in range(EARLY):
                base = ROUNDS_FIRST + b * EARLY_ROUNDS
                w_count = used_before(0, b)
                with pe.Fori(0, NODE_TILES // 2 - 1) as jj:
                    for bank in range(2):
                        count_round(base + 2 * jj + bank,
                                    messages(0, b, 2 * jj + bank, bank, P, w_count, RING - 1))
                for j in range(NODE_TILES - 2, NODE_TILES):
                    count_round(base + j, messages(0, b, j, j % 2, P if j < NODE_TILES - 1 else LAST_ROWS,
                                                   w_count, RING - 1))
                if b:
                    pe.wait_ge(root_taken, b)
                base += NODE_TILES
                def root_passes(k, first, final):
                    return [lambda n=n: root_pass(0, k, n, first, final) for n in range(RING - 1)]

                count_round(base, root_passes(0, True, False))
                with pe.Fori(1, K_TILES[0] - 1) as k:
                    count_round(base + k, root_passes(k, False, False))
                last_passes = root_passes(K_TILES[0] - 1, False, True)
                last_passes[-1] = lambda: root_pass(0, K_TILES[0] - 1, 2, False, True).then_inc(root_ready, 1)
                count_round(base + K_TILES[0] - 1, last_passes)
                base += K_TILES[0]
                with pe.Fori(base, base + ROUNDS_SPLIT if b < EARLY - 1 else ROUNDS) as it:
                    count_round(it)
            most = pe.value_load(most_i, min_val=0, max_val=N // WIN)
            with pe.If(most > 0):
                with pe.Fori(0, GROUPS * most) as v:
                    pe.wait_ge(far_hot, v + 1)
                    count(0, 0).then_inc(far_counted, 1)

            pe.wait_ge(counts_done, 1)
            pe.wait_ge(root_taken, EARLY)
            for r in range(RELS):
                if r == 2:
                    pe.wait_ge(degrees_taken, 1)
                for j in range(NODE_TILES):
                    for c, (c0, cw) in enumerate(CHUNKS):
                        last = M.matmul(trio[:, r % 2, c, 0:cw], ones_h[:], counts[:, j, r, c0:c0 + cw],
                                        start=(j == 0), stop=(j == NODE_TILES - 1))
                last.then_inc(degrees_ready, 1)
            pe.wait_ge(degrees_taken, RELS)
            for b in range(EARLY):
                gathering(b, early_msgs[b])
            for l in range(LAYERS):
                if l:
                    pe.wait_ge(block_done, FIRST[l] + DONE_CREDIT)
                if l == LAST:
                    pe_block(l, 0, False)
                with pe.Fori(START[l], T[l]) as t:
                    pe_block(l, t, l == LAST)
            turn_out(T[LAST] - 1)


_INS = ['x', 'src', 'dst', 'edge_type_3', 'node_type_3', 'L0_gnn_node_emb', 'L0_gnn_w_rel1', 'L0_gnn_w_root1',
        'L0_gnn_b1', 'L0_gnn_w_rel2', 'L0_gnn_w_root2', 'L0_gnn_b2', 'L0_gnn_w_rel3', 'L0_gnn_w_root3', 'L0_gnn_b3']
_OUTS = [((N, 768), 'float32')]


def kernel(**inputs):
    import numpy as _np
    import concourse.bacc as _bacc
    from concourse import mybir as _mybir
    from concourse.bass_utils import run_bass_kernel_spmd as _run

    nc = _bacc.Bacc("TRN2", target_bir_lowering=False, num_devices=1)
    arrays, args = {}, []
    for name in _INS:
        a = _np.ascontiguousarray(inputs[name])
        arrays[f"in_{name}_dram"] = a
        args.append(nc.dram_tensor(f"in_{name}_dram", a.shape, _mybir.dt.from_np(a.dtype), kind="ExternalInput").ap())
    for i, (shape, dtype) in enumerate(_OUTS):
        dt = _mybir.dt.from_np(_np.dtype(dtype))
        args.append(nc.dram_tensor(f"out_{i}_dram", shape, dt, kind="ExternalOutput").ap())
    gnn_kernel(nc, *args)
    r = _run(nc, [arrays], core_ids=[0])
    got = tuple(r.results[0][f"out_{i}_dram"] for i in range(len(_OUTS)))
    return got[0]
```

```python
from contextlib import ExitStack

import concourse.bass as bass
from concourse import mybir


P = 128
N = 1250
NODE_TILES = (N + P - 1) // P
FULL_ROWS = (NODE_TILES - 1) * P
LAST_ROWS = N - FULL_ROWS
IN_CH = 768
TYPE_DIM = 128
RELS = 3
MATS = RELS + 1
EDGES = 40000
K_TILES = (7, 7, 6)
T = (7, 6, 6)
LAYERS = 3
TYPES = 3
LO_ROW = 32
EMB_ROWS = LO_ROW + TYPES
EMB_COLS = 64
FULL_TILES = (IN_CH // P, 7, 6)
FIRST = (0, T[0], T[0] + T[1])
BLOCKS = sum(T)

CHUNKS = ((0, 417), (417, 417), (834, 416))
CHUNK = 417
BANK = 512
H0_CHUNKS = tuple((c, min(BANK, N - c)) for c in range(0, N, BANK))

SUB = 125
SUBS = 2
GROUPS = EDGES // (SUB * SUBS)
HALVES = 2
GP = GROUPS // HALVES
HE = EDGES // GP
WIN = 12
WIN_COLS = NODE_TILES * RELS * WIN
N_PAD = 1264
LAST_WIN = N_PAD - WIN
RING = 4
ACT_SLOTS = (3,)
FAR_STEPS = 7
DVE_NORMS = 7
ZEROED_FIRST = 4
X_FIRST = 4
SCANS0 = K_TILES[0]
SCAN_HALVINGS = 2
SCANS_BEFORE = 3
EARLY = 2
ROUNDS = GROUPS // RING
ROUNDS_FIRST = 3
ROUNDS_SPLIT = 2
EARLY_ROUNDS = NODE_TILES + K_TILES[0] + ROUNDS_SPLIT

TINY = 1e-30
EXPONENT = 0x7F800000
INVERSE_BITS = float(254 << 23)
TOP = 2.0 ** 14
TOP_EMB = 2.0 ** 7
HOT = 2.0 ** 15
K_BOUND = 1024.0
LN_BOUND = 27.8
EPS = 1e-5

F32 = mybir.dt.float32
F16 = mybir.dt.float16
BF16 = mybir.dt.bfloat16
I32 = mybir.dt.int32
ALU = mybir.AluOpType
ACT = mybir.ActivationFunctionType
AX = mybir.AxisListType
RMAX = bass.bass_isa.ReduceOp.max

RING_CREDIT = RING
BANK_CREDIT = 2
SLOT_CREDIT = 4
STORE_CREDIT = 64
RESID_CREDIT = 32
DONE_CREDIT = 1
SRC_CREDIT = 1
SRC_B_CREDIT = 1

SCAN_INC = 2 * 16
OWN_INC = MATS * 16
OWN0 = 2
IN0 = 2 * OWN_INC
LAST = LAYERS - 1
START = (EARLY, 0, 1)
ROOT_SET = 1


def used_before(l, t):
    return OWN0 + 4 * (FIRST[l] + t) if l < LAST else OWN0 + 4 * FIRST[l] + 2 * t


def in_before(l, t):
    block = 2 * (SCAN_INC + OWN_INC)
    return IN0 + block * (FIRST[l] + t) if l < LAST else IN0 + block * FIRST[l] + 2 * OWN_INC * t


def scans(l):
    return 2 if l < LAST else 0


def w_scaled_at(l):
    return 2 + 2 * l


def m_scaled_at(l):
    return 3 + 2 * l


class Steps:

    def __init__(self, eng, semaphore):
        self.eng, self.semaphore, self.base, self.count = eng, semaphore, 0, 0

    def then(self, instruction):
        self.count += 1
        instruction.then_inc(self.semaphore, 1)
        self.eng.wait_ge(self.semaphore, self.base + self.count)


def gnn_kernel(nc, x, src, dst, edge_type, node_type, node_emb,
               w_rel1, w_root1, b1, w_rel2, w_root2, b2, w_rel3, w_root3, b3, out):
    bias = (b1, b2, b3)
    mats = tuple([wr[0], wr[1], wr[2], wo] for wr, wo in
                 ((w_rel1, w_root1), (w_rel2, w_root2), (w_rel3, w_root3)))

    with ExitStack() as ctx:
        def sb(name, shape, dt):
            return ctx.enter_context(nc.sbuf_tensor(name, shape, dt))

        def sem(name):
            return ctx.enter_context(nc.semaphore(name))

        counts = sb("counts", [P, NODE_TILES, RELS, N_PAD], F16)
        h_a = sb("h_a", [P, 2, 7, N], F16)
        h_b = sb("h_b", [P, 2, 7, N], F16)
        h_in = (h_a, h_b, h_a)
        msg = sb("msg", [P, NODE_TILES, 2, RELS * P], F16)
        w_split = sb("w_split", [P, 7, 2, MATS, P], F16)
        w_raw = sb("w_raw", [P, 4 * MATS * P], F32)
        inv = sb("inv", [P, RELS, N], F32)
        acc = sb("acc", [P, N], F32)
        acc_b = sb("acc_b", [P, N], F32)
        ones_h = sb("ones_h", [P, P], F16)
        one = sb("one", [P, 1], F32)
        part = sb("part", [P, CHUNK], F32)
        ident = sb("ident", [P, P], F32)
        bias_sb = sb("bias_sb", [P, BLOCKS], F32)
        W_MAX, W_SCALE, W_BACK, H_TOP, H_SCALE, H_BACK, M_SCALE, M_BACK, ROOT_BACK, REL_BACK, B1, B2 = range(12)
        sc = sb("sc", [P, LAYERS, 12], F32)
        tile_max = sb("tile_max", [P, 3 * T[0]], F32)
        local = sb("local", [P, 2], F32)
        over_all = sb("over_all", [P, 2], F32)
        bias_max = sb("bias_max", [P, 1], F32)

        flat_a = h_a[:].rearrange("p a k n -> p (a k n)").bitcast(F32)
        flat_b = h_b[:].rearrange("p a k n -> p (a k n)").bitcast(F32)
        flat_w = w_split[:].rearrange("p k a m e -> p (k a m e)").bitcast(F32)
        flat_m = msg[:].rearrange("p j a e -> p (j a e)")
        flat_mf = flat_m.bitcast(F32)
        flat_i = inv[:].rearrange("p r n -> p (r n)")
        x_sb = flat_b[:, 0:NODE_TILES * IN_CH].rearrange("p (j c) -> p j c", j=NODE_TILES)

        def rows_of(k, n=1):
            return flat_a[0:GP, k * HE:(k + n) * HE]

        ed = rows_of(0, 3).bitcast(I32).rearrange("p (a h i) -> p a h i", a=3, h=HALVES)
        src_hi = rows_of(3).bitcast(I32)
        src_lo = rows_of(4).bitcast(I32)
        keys = rows_of(5, 4).rearrange("p (a h u i) -> p a h u i", a=4, h=HALVES, u=SUBS)
        key_tmp = rows_of(9)
        lowest = flat_a[0:GP, 10 * HE:10 * HE + HALVES]
        highest = flat_a[0:GP, 10 * HE + 2:10 * HE + 2 + HALVES]
        extra = flat_a[0:GP, 10 * HE + 4:10 * HE + 4 + HALVES]
        msg_b = [flat_h[:, at:at + NODE_TILES * RELS * P].rearrange("p (j e) -> p j e", j=NODE_TILES)
                 for flat_h in (h_b[:].rearrange("p a k n -> p (a k n)"),) for at in (2 * N, 9 * N)]
        msgs_a = (msg[:, :, 0, :], msg[:, :, 1, :])
        early_msgs, early_accs = (msgs_a, msg_b), (acc, acc_b)
        stats = part[:, P:P + 120].rearrange("p (j s) -> p j s", j=NODE_TILES)
        mean_var = part[:, 250:270].rearrange("p (j s) -> p j s", j=NODE_TILES)
        var_eps, std, rstd, newton, newton2 = (part[:, 270 + 10 * k:280 + 10 * k] for k in range(5))
        emb = part[0:TYPES, 0:TYPE_DIM]
        emb_scaled = part[:, 330:330 + TYPES]
        hot_type = h_a[:, 0, FULL_TILES[0], :]
        emb_w = h_a[0:EMB_COLS, 1, FULL_TILES[0], 0:MATS * P]
        emb_t = h_a[:, 1, FULL_TILES[0], MATS * P:MATS * P + 2 * EMB_COLS].rearrange("p (a e) -> p a e", a=2)
        bias_rows = w_raw[0:BLOCKS, 0:P]
        iota_i = w_raw[:, P:P + WIN_COLS].bitcast(I32)
        part_id_i = w_raw[:, 600:601].bitcast(I32)
        part_id = w_raw[:, 602:603]
        row_f = w_raw[0:1, 640:640 + 2 * GROUPS].rearrange("p (a g) -> p a g", a=2)
        most_f = w_raw[0:1, 1000:1001]
        type_i = acc[0:EMB_ROWS, :].bitcast(I32)
        scan_bufs = (flat_mf[:, 0:MATS * T[0] * P], flat_w[:, 0:MATS * T[0] * P])
        flat_ih = flat_i.bitcast(F16)
        ring_main = flat_ih[:, 0:RING * SUBS * WIN_COLS].rearrange("p (s u c) -> p s u c", s=RING, u=SUBS)
        ring_src = flat_ih[:, RING * SUBS * WIN_COLS:RING * SUBS * (WIN_COLS + P)].rearrange(
            "p (s u c) -> p s u c", s=RING, u=SUBS)
        used = RING * SUBS * (WIN_COLS + P) // 2
        keys_t = flat_i[0:SUB, used:used + 4 * SUBS * GROUPS].rearrange("p (a u g) -> p a u g", a=4, u=SUBS)
        used += 4 * SUBS * GROUPS
        iota_h = flat_i[:, used:used + WIN_COLS // 2].bitcast(F16)
        used += WIN_COLS // 2
        row_i = flat_i[0:1, used:used + GROUPS].bitcast(I32)
        used += GROUPS
        most_i = flat_i[0:1, used:used + 1].bitcast(I32)
        far = flat_i[0:SUB, used + 2:used + 10]
        ring_keys = flat_i[0:SUB, used + 10:used + 10 + RING]
        gate = flat_i[0:SUB, used + 14:used + 15 + RING]
        assert used + 15 + RING <= RELS * N
        scan_row = flat_i.bitcast(BF16)[:, 0:MATS * T[0] * P]
        scan_half = acc_b[:].bitcast(BF16)[:, 0:MATS * T[0] * P // 2]
        src_squares = part[0:SUB, 0:RING * P // 2].bitcast(F16).rearrange("p (s c) -> p s c", s=RING)
        resid = flat_b[:, 0:2 * NODE_TILES * P].rearrange("p (s j c) -> p s j c", s=2, j=NODE_TILES)

        pair = ctx.enter_context(nc.psum_tensor("pair", [P, 2, BANK], F32))
        trio = ctx.enter_context(nc.psum_tensor("trio", [P, 2, 3, BANK], F32))

        edges_in, x_first_in, x_in, small_in = sem("edges_in"), sem("x_first_in"), sem("x_in"), sem("small_in")
        consts_made, counts_zeroed = sem("consts_made"), sem("counts_zeroed")
        keys_made, keys_turned, keys_kept = sem("keys_made"), sem("keys_turned"), sem("keys_kept")
        rows_made, rows_kept = sem("rows_made"), sem("rows_kept")
        main_hot, src_hot, ring_keyed = sem("main_hot"), sem("src_hot"), sem("ring_keyed")
        src_squared, src_hot_b = sem("src_squared"), sem("src_hot_b")
        col_far, act_hot = sem("col_far"), sem("act_hot")
        group_counted, group_added = sem("group_counted"), sem("group_added")
        far_hot, far_counted, far_added = sem("far_hot"), sem("far_counted"), sem("far_added")
        counts_done = sem("counts_done")
        degrees_ready, degrees_taken, inverted = sem("degrees_ready"), sem("degrees_taken"), sem("inverted")
        var_ready, std_ready, stats_ready, x_normed = sem("var_ready"), sem("std_ready"), sem("stats_ready"), sem("x_normed")
        h0_ready, h0_hi, h0_lo = sem("h0_ready"), sem("h0_hi"), sem("h0_lo")
        emb_ready, emb_hi, emb_split = sem("emb_ready"), sem("emb_hi"), sem("emb_split")
        scan_in = (sem("scan_in_a"), sem("scan_in_b"))
        scan_abs, scan_halved, scans_done = sem("scan_abs"), sem("scan_halved"), sem("scans_done")
        w_in, w_hi, w_used = sem("w_in"), sem("w_hi"), sem("w_used")
        max_local, max_over_all, scales_ready = sem("max_local"), sem("max_over_all"), sem("scales_ready")
        msg_ready, msg_hi, msg_split = sem("msg_ready"), sem("msg_hi"), sem("msg_split")
        root_ready, root_taken = sem("root_ready"), sem("root_taken")
        rel_ready, rel_taken, rel_added = sem("rel_ready"), sem("rel_taken"), sem("rel_added")
        h_scaled, h_hi, block_done = sem("h_scaled"), sem("h_hi"), sem("block_done")
        resid_in, out_turned, out_added, stored = sem("resid_in"), sem("out_turned"), sem("out_added"), sem("stored")
        bias_turned = sem("bias_turned")
        dve_step, far_step = sem("dve_step"), sem("far_step")

        def own_view(l, half):
            ks = 4 if half == 0 else K_TILES[l] - 4
            return ks, w_raw[:, 0:ks * MATS * P]

        def normalise(eng, j):
            rows = P if j < NODE_TILES - 1 else LAST_ROWS
            return eng.tensor_scalar(x_sb[0:rows, j, :], x_sb[0:rows, j, :], mean_var[0:rows, j, 0:1],
                                     rstd[0:rows, j:j + 1], ALU.subtract, ALU.mult)

        block = ctx.enter_context(nc.Block())

        @block.sync
        def _(sp):
            for a, arr in enumerate((dst, src, edge_type)):
                sp.dma_start(ed[:, a], arr.rearrange("(h p i) -> p h i", h=HALVES, p=GP)
                             ).then_inc(edges_in, 16)
            for r in [at + n for at in (0, LO_ROW) for n in range(TYPES)]:
                sp.dma_start(type_i[r:r + 1, :], node_type.rearrange("(a n) -> a n", a=1)
                             ).then_inc(small_in, 16)
            sp.dma_start(emb, node_emb).then_inc(small_in, 16)
            for l in range(LAYERS):
                sp.dma_start(bias_rows[FIRST[l]:FIRST[l] + T[l], :],
                             bias[l].rearrange("(t p) -> t p", p=P)).then_inc(small_in, 16)
            sp.dma_start(x_sb[:, 0:X_FIRST, :],
                         x[0:X_FIRST * P, :].rearrange("(j p) c -> p j c", p=P)).then_inc(x_first_in, 16)
            sp.dma_start(x_sb[:, X_FIRST:NODE_TILES - 1, :],
                         x[X_FIRST * P:FULL_ROWS, :].rearrange("(j p) c -> p j c", p=P)).then_inc(x_in, 16)
            sp.dma_start(x_sb[0:LAST_ROWS, NODE_TILES - 1, :], x[FULL_ROWS:N, :]).then_inc(x_in, 16)

            def load_scan(l, kt, half):
                cols = T[l] * P
                for q in range(2):
                    sp.dma_start(w_raw[:, q * cols:(q + 1) * cols],
                                 mats[l][2 * half + q][bass.ds(kt * P, P), :]).then_inc(w_in, 16)

            def load_own(l, t, half):
                ks, raw = own_view(l, half)
                view = raw.rearrange("p (k m e) -> p k m e", k=ks, m=MATS)
                for m in range(MATS):
                    rows = mats[l][m][half * 4 * P:(half * 4 + ks) * P, bass.ds(t * P, P)]
                    sp.dma_start(view[:, :, m, :], rows.rearrange("(k p) e -> p k e", p=P)
                                 ).then_inc(w_in, 16)

            for n in range(SCANS0):
                if n >= 2:
                    sp.wait_ge(scan_abs, n - 1)
                for m in range(MATS):
                    sp.dma_start(scan_bufs[n % 2][:, m * T[0] * P:(m + 1) * T[0] * P],
                                 mats[0][m][n * P:(n + 1) * P, :]).then_inc(scan_in[n % 2], 16)
            sp.wait_ge(rows_kept, 1)
            load_own(0, 0, 0)
            sp.wait_ge(w_used, 1)
            load_own(0, 0, 1)

            def block_loads(l, t, next_l, next_t):
                before = used_before(l, t)
                for half in range(scans(l)):
                    sp.wait_ge(w_used, before + half)
                    load_scan(l + 1, t, half)
                if l == LAST:
                    slot = sp.snap(t % 2)
                    sp.wait_ge(stored, 32 * t + STORE_CREDIT - 32)
                    sp.wait_ge(resid_in, 32 * t + RESID_CREDIT)
                    for j0, nj, rows in ((0, NODE_TILES - 1, P), (NODE_TILES - 1, 1, LAST_ROWS)):
                        sp.dma_start(
                            resid[0:rows, bass.ds(slot, 1), j0:j0 + nj, :].rearrange("p s j c -> p (s j) c"),
                            x[j0 * P:j0 * P + nj * rows, bass.ds(t * P, P)].rearrange("(j p) c -> p j c", p=rows)
                        ).then_inc(resid_in, 16)
                if next_l is not None:
                    for half in range(2):
                        sp.wait_ge(w_used, before + scans(l) + half)
                        load_own(next_l, next_t, half)

            for l in range(LAYERS):
                if l == LAST:
                    sp.wait_ge(msg_ready, NODE_TILES * FIRST[LAST])
                with sp.Fori(0, T[l] - 1) as t:
                    block_loads(l, t, l, t + 1)
                block_loads(l, T[l] - 1, l + 1 if l < LAST else None, 0)

        @block.gpsimd
        def _(pool):
            pool.iota(iota_i, [[1, WIN_COLS]], base=0, channel_multiplier=0).then_inc(consts_made, 1)
            pool.iota(part_id_i, [[0, 1]], base=0, channel_multiplier=1).then_inc(consts_made, 1)
            pool.memset(ident[:], 1.0).then_inc(consts_made, 1)
            pool.wait_ge(consts_made, 3)
            pool.affine_select(out=ident[:], in_=ident[:], compare_op=ALU.is_equal, fill=0.0, base=0,
                               pattern=[[-1, P]], channel_multiplier=1).then_inc(consts_made, 1)
            pool.memset(ones_h[:], 1.0).then_inc(consts_made, 1)
            pool.memset(one[:], 1.0).then_inc(consts_made, 1)

            def join(n):
                pool.wait_ge(max_local, n)
                pool.partition_all_reduce(over_all[:], local[:], P, RMAX).then_inc(max_over_all, 1)

            join(1)
            pool.memset(counts[:, 0:ZEROED_FIRST], 0.0).then_inc(counts_zeroed, 1)
            pool.wait_ge(stats_ready, 1)
            for j in range(DVE_NORMS, NODE_TILES):
                normalise(pool, j).then_inc(x_normed, 1)
            pool.memset(counts[:, ZEROED_FIRST:], 0.0).then_inc(counts_zeroed, 1)
            join(2)
            pool.wait_ge(keys_kept, 2)
            with pool.Fori(0, GROUPS // RING) as it:
                pool.wait_ge(src_hot, it * RING + SRC_CREDIT)
                pool.tensor_copy(ring_keys, keys_t[:, 1, 0, bass.ds(it * RING, RING)]).then_inc(ring_keyed, 1)
                pool.wait_ge(ring_keyed, it + 1)
                pool.tensor_tensor(gate[:, RING:RING + 1], ident[0:SUB, 0:1], ident[0:SUB, 0:1], ALU.mult)
                for slot in range(RING):
                    g = it * RING + slot
                    pool.wait_ge(group_counted, g + RING_CREDIT - RING + 1)
                    pool.tensor_tensor(gate[:, slot:slot + 1], ident[0:SUB, 0:1], ident[0:SUB, 0:1], ALU.mult)
                    pool.tensor_scalar(ring_src[0:SUB, slot, 0, :], iota_h[0:SUB, 0:P],
                                       ring_keys[:, slot:slot + 1], None, ALU.is_equal).then_inc(src_hot, 1)
            for n in range(3, 7):
                join(n)

        @block.scalar
        def _(act):
            for a in range(4):
                act.wait_ge(keys_turned, a + 1)
                nc.scalar.activation(keys_t[:, a], trio[0:SUB, a % 2, a // 2, 0:SUBS * GROUPS].rearrange(
                    "p (u g) -> p u g", u=SUBS), ACT.Copy).then_inc(keys_kept, 1)
            act.wait_ge(var_ready, 1)
            nc.scalar.activation(std, var_eps, ACT.Sqrt).then_inc(std_ready, 1)

            def scan_magnitudes(n):
                act.wait_ge(scan_in[n % 2], (n // 2 + 1) * MATS * 16)
                if n:
                    act.wait_ge(scan_halved, n)
                nc.scalar.activation(scan_row, scan_bufs[n % 2], ACT.Abs).then_inc(scan_abs, 1)

            for n in range(SCANS_BEFORE):
                scan_magnitudes(n)
            for k in range(FULL_TILES[0]):
                act.wait_ge(h0_ready, k + 1)
                for c, (c0, cw) in enumerate(H0_CHUNKS):
                    last = nc.scalar.activation(h_a[:, 0, k, c0:c0 + cw], trio[:, k % 2, c, 0:cw],
                                                ACT.Relu)
                last.then_inc(h0_hi, 1)
                if k + SCANS_BEFORE < SCANS0:
                    scan_magnitudes(k + SCANS_BEFORE)

            def split_w(l, t, half, in_count):
                ks, raw = own_view(l, half)
                act.wait_ge(w_in, in_count)
                nc.scalar.activation(
                    w_split[:, 4 * half:4 * half + ks, 0].rearrange("p k m e -> p k (m e)"),
                    raw.rearrange("p (k e) -> p k e", k=ks), ACT.Copy, scale=sc[:, l, W_SCALE:W_SCALE + 1]
                ).then_inc(w_hi, 1)

            def source_rows(it, between=None):
                act.wait_ge(src_hot_b, it * RING + SRC_B_CREDIT)
                for slot in range(RING):
                    g = it * RING + slot
                    nc.scalar.activation(src_squares[:, slot, :], iota_h[0:SUB, 0:P], ACT.Square, scale=-1.0,
                                         bias=keys_t[:, 1, 1, bass.ds(g, 1)]).then_inc(src_squared, 1)
                for slot in range(RING):
                    g = it * RING + slot
                    if slot == RING - 1 and between is not None:
                        between()
                    act.wait_ge(src_squared, g + 1)
                    act.wait_ge(group_counted, g + RING_CREDIT - RING + 1)
                    row = ring_main[0:SUB, slot, SUBS - 1, :]
                    if slot in ACT_SLOTS:
                        nc.scalar.activation(row, iota_h[0:SUB, :], ACT.Abs, scale=-1.0,
                                             bias=keys_t[:, 0, SUBS - 1, bass.ds(g, 1)]).then_inc(col_far, 1)
                    nc.scalar.activation(ring_src[0:SUB, slot, 1, :], src_squares[:, slot, :], ACT.Relu, scale=-1.0,
                                         bias=one[0:SUB]).then_inc(src_hot_b, 1)
                    if slot in ACT_SLOTS:
                        act.wait_ge(col_far, len(ACT_SLOTS) * it + ACT_SLOTS.index(slot) + 1)
                        nc.scalar.activation(row, row, ACT.Relu, scale=-1.0, bias=one[0:SUB]).then_inc(act_hot, 1)

            act.wait_ge(scales_ready, w_scaled_at(0))
            split_w(0, 0, 0, OWN_INC)
            for n in range(ROUNDS_FIRST):
                source_rows(n)
            split_w(0, 0, 1, IN0)
            source_rows(ROUNDS_FIRST)

            def store(t):
                act.wait_ge(out_added, t + 1)
                act.wait_ge(stored, 32 * t + STORE_CREDIT)
                slot = act.snap(t % 2)
                for j0, nj, rows in ((0, NODE_TILES - 1, P), (NODE_TILES - 1, 1, LAST_ROWS)):
                    act.dma_start(
                        out[j0 * P:j0 * P + nj * rows, bass.ds(t * P, P)].rearrange("(j p) c -> p j c", p=rows),
                        resid[0:rows, bass.ds(slot, 1), j0:j0 + nj, :].rearrange("p s j c -> p (s j) c")
                    ).then_inc(stored, 16)

            def high_embeddings(g):
                act.wait_ge(emb_ready, g + 1)
                nc.scalar.activation(emb_w, pair[0:EMB_COLS, 1, 0:MATS * P], ACT.Copy,
                                     scale=1.0 / HOT).then_inc(emb_hi, 1)

            def high_message(l, g, j, bank, rows, msgs):
                act.wait_ge(msg_ready, NODE_TILES * g + j + 1)
                nc.scalar.activation(msgs[0][0:rows, bass.ds(j, 1), :].rearrange("p j e -> p (j e)"),
                                     pair[0:rows, bank, 0:RELS * P], ACT.Copy,
                                     scale=sc[0:rows, l, M_SCALE:M_SCALE + 1]).then_inc(msg_hi, 1)

            def high_messages(l, g, msgs):
                for j in range(NODE_TILES):
                    high_message(l, g, j, j % 2, P if j < NODE_TILES - 1 else LAST_ROWS, msgs)

            def take_root(l, g, to, from_set=ROOT_SET):
                act.wait_ge(root_ready, g + 1)
                for c, (c0, cw) in enumerate(CHUNKS):
                    last = nc.scalar.activation(to[:, c0:c0 + cw], trio[:, from_set, c, 0:cw], ACT.Identity,
                                                bias=bias_sb[:, bass.ds(g, 1)],
                                                scale=sc[:, l, ROOT_BACK:ROOT_BACK + 1])
                last.then_inc(root_taken, 1)

            def split_next(l, t, next_l, next_t):
                act.wait_ge(scales_ready, w_scaled_at(next_l))
                for half in range(2):
                    split_w(next_l, next_t, half, in_before(l, t) + scans(l) * SCAN_INC + (half + 1) * OWN_INC)

            def high_h(l, t, done):
                act.wait_ge(h_scaled, FIRST[l] + t + 1)
                nc.scalar.activation(h_in[l + 1][:, 0, bass.ds(t, 1), :].rearrange("p k n -> p (k n)"),
                                     done[:], ACT.Copy).then_inc(h_hi, 1)

            def act_block(l, t, next_l, next_t, stores):
                g = FIRST[l] + t
                if l == 0:
                    high_embeddings(g)
                high_messages(l, g, msgs_a)
                if stores:
                    store(t - 1)
                if l < LAST:
                    act.wait_ge(block_done, g + DONE_CREDIT)
                take_root(l, g, acc)
                if next_l is not None:
                    split_next(l, t, next_l, next_t)
                if l < LAST:
                    high_h(l, t, acc)

            for l in range(LAYERS):
                act.wait_ge(scales_ready, m_scaled_at(l))
                if l == 0:
                    for b in range(EARLY):
                        ahead = ROUNDS_FIRST + b * EARLY_ROUNDS + 1
                        high_embeddings(b)
                        with act.Fori(0, NODE_TILES // 2 - 1) as jj:
                            for bank in range(2):
                                source_rows(ahead + 2 * jj + bank, lambda: high_message(
                                    0, b, 2 * jj + bank, bank, P, early_msgs[b]))
                        for j in range(NODE_TILES - 2, NODE_TILES):
                            source_rows(ahead + j, lambda: high_message(
                                0, b, j, j % 2, P if j < NODE_TILES - 1 else LAST_ROWS, early_msgs[b]))
                        ahead += NODE_TILES
                        with act.Fori(ahead, ahead + K_TILES[0]) as it:
                            source_rows(it)
                        ahead += K_TILES[0]
                        take_root(0, b, early_accs[b], 0)
                        if b:
                            high_h(0, b - 1, early_accs[b - 1])
                        for half in range(2):
                            split_w(0, b + 1, half, in_before(0, b) + scans(0) * SCAN_INC + (half + 1) * OWN_INC)
                            if b < EARLY - 1:
                                source_rows(ahead + half)
                    high_h(0, EARLY - 1, early_accs[EARLY - 1])
                if l == LAST:
                    act.wait_ge(block_done, FIRST[LAST] + DONE_CREDIT)
                    act_block(l, 0, l, 1, False)
                with act.Fori(START[l], T[l] - 1) as t:
                    act_block(l, t, l, t + 1, l == LAST)
                act_block(l, T[l] - 1, l + 1 if l < LAST else None, 0, l == LAST)
            store(T[LAST] - 1)
            act.wait_ge(stored, 32 * T[LAST] + STORE_CREDIT)

        @block.vector
        def _(dve):
            steps = Steps(dve, dve_step)
            then = steps.then
            V = nc.vector

            dve.wait_ge(edges_in, 48)
            d_i = ed[:, 0]
            src_f = ed[:, 1].rearrange("p h i -> p (h i)")
            rel_f = ed[:, 2].rearrange("p h i -> p (h i)")
            flat = [keys[:, a].rearrange("p h u i -> p (h u i)") for a in range(4)]
            V.tensor_scalar(src_hi, src_f, 7, None, ALU.logical_shift_right)
            V.tensor_scalar(src_lo, src_f, P - 1, None, ALU.bitwise_and)
            V.tensor_reduce(highest, d_i, AX.X, ALU.max)
            then(V.tensor_reduce(lowest, d_i, AX.X, ALU.min))
            for h in range(HALVES):
                V.tensor_scalar(keys[:, 3, h].rearrange("p u i -> p (u i)"), d_i[:, h, :], lowest[:, h:h + 1],
                                None, ALU.subtract)
            V.tensor_copy(flat[1], src_lo)
            V.tensor_tensor(extra, highest, lowest, ALU.subtract)
            then(V.tensor_scalar(key_tmp, rel_f, float(WIN), 1.0, ALU.mult, ALU.add))
            then(V.scalar_tensor_tensor(out=flat[2], in0=src_hi, scalar=float(RELS * WIN), in1=key_tmp,
                                        op0=ALU.mult, op1=ALU.add))
            then(V.tensor_scalar(extra, extra, 0.5, 1.0 / WIN, ALU.add, ALU.mult))
            then(V.tensor_scalar(extra, extra, -0.5, None, ALU.add))
            then(V.tensor_tensor(key_tmp, flat[2], flat[3], ALU.add))
            then(V.scalar_tensor_tensor(out=key_tmp, in0=flat[3], scalar=float(WIN), in1=key_tmp,
                                        op0=ALU.is_lt, op1=ALU.mult))
            V.tensor_scalar(flat[0], key_tmp, -1.0, None, ALU.add).then_inc(keys_made, 1)

            dve.wait_ge(small_in, 16 * (2 * TYPES + 1 + LAYERS))
            dve.wait_ge(consts_made, 6)
            dve.wait_ge(bias_turned, 1)
            then(V.tensor_copy(bias_sb[:], pair[:, 1, 0:BLOCKS]))
            V.tensor_copy(iota_h, iota_i)
            then(V.tensor_scalar(part_id_i, part_id_i, LO_ROW - 1, None, ALU.bitwise_and))
            V.tensor_copy(part_id, part_id_i)
            then(V.memset(local[:], 0.0))
            V.tensor_reduce(local[0:TYPES, 0:1], emb, AX.X, ALU.max, apply_absolute_value=True)
            V.tensor_reduce(local[:, 1:2], bias_sb[:], AX.X, ALU.max,
                            apply_absolute_value=True).then_inc(max_local, 1)

            def c_(l, k):
                return sc[:, l, k:k + 1]

            def scale_of(l, bound, scale, back, top=TOP):
                then(V.tensor_scalar(c_(l, back).bitcast(I32), c_(l, bound).bitcast(I32), EXPONENT, None,
                                     ALU.bitwise_and))
                then(V.tensor_scalar(c_(l, scale).bitcast(I32), c_(l, back).bitcast(I32), -1.0, INVERSE_BITS,
                                     ALU.mult, ALU.add))
                V.tensor_scalar(c_(l, scale), c_(l, scale), top, None, ALU.mult)
                return V.tensor_scalar(c_(l, back), c_(l, back), 1.0 / top, None, ALU.mult)

            dve.wait_ge(max_over_all, 1)
            V.tensor_copy(bias_max[:], over_all[:, 1:2])
            then(V.tensor_scalar(c_(0, B1), over_all[:, 0:1], LN_BOUND, None, ALU.max))
            then(scale_of(0, B1, H_SCALE, H_BACK))
            then(V.tensor_tensor(c_(0, H_TOP), c_(0, B1), c_(0, H_SCALE), ALU.mult))
            V.tensor_copy(local[:, 0:1], c_(0, H_TOP)).then_inc(scales_ready, 1)
            V.memset(emb_t, 0.0)
            then(V.tensor_scalar(emb_scaled, pair[:, 1, EMB_COLS:EMB_COLS + TYPES], c_(0, H_SCALE), None, ALU.mult))
            for at in (0, LO_ROW):
                ins = V.tensor_copy(emb_t[:, 0, at:at + TYPES], emb_scaled)
            then(ins)
            for at in (0, LO_ROW):
                V.tensor_tensor(emb_t[:, 1, at:at + TYPES], emb_scaled, emb_t[:, 0, at:at + TYPES], ALU.subtract)

            def scan_first(n):
                dve.wait_ge(scan_abs, n + 1)
                width = MATS * T[0] * P // 2
                V.tensor_tensor(scan_half, scan_row[:, 0:width], scan_row[:, width:2 * width],
                                ALU.max).then_inc(scan_halved, 1)
                dve.wait_ge(scan_halved, n + 1)
                for _ in range(SCAN_HALVINGS):
                    width //= 2
                    then(V.tensor_tensor(scan_half[:, 0:width], scan_half[:, 0:width],
                                         scan_half[:, width:2 * width], ALU.max))
                ins = V.tensor_reduce(tile_max[:, n:n + 1], scan_half[:, 0:width], AX.X, ALU.max)
                if n < SCANS0 - 1:
                    then(ins)
                else:
                    ins.then_inc(scans_done, 1)

            dve.wait_ge(x_first_in, 16)
            for j in range(NODE_TILES):
                if j == X_FIRST:
                    dve.wait_ge(x_in, 32)
                rows = P if j < NODE_TILES - 1 else LAST_ROWS
                for s in range(2):
                    V.bn_stats(stats[0:rows, j, 6 * s:6 * s + 6], x_sb[0:rows, j, 384 * s:384 * s + 384])
            if LAST_ROWS < P:
                V.memset(mean_var[:, NODE_TILES - 1, :], 1.0)
            then(V.tensor_copy(local[:, 1:2], bias_max[:]))
            for j in range(NODE_TILES):
                rows = P if j < NODE_TILES - 1 else LAST_ROWS
                ins = V.bn_aggr(mean_var[0:rows, j, :], stats[0:rows, j, :])
            then(ins)
            V.tensor_scalar(var_eps, mean_var[:, :, 1], EPS, None, ALU.add).then_inc(var_ready, 1)
            dve.wait_ge(std_ready, 1)
            then(V.reciprocal(rstd, std))
            then(V.tensor_tensor(newton, rstd, rstd, ALU.mult))
            then(V.tensor_tensor(newton2, newton, var_eps, ALU.mult))
            then(V.tensor_scalar(newton, newton2, -0.5, 1.5, ALU.mult, ALU.add))
            then(V.tensor_tensor(newton2, newton, rstd, ALU.mult))
            V.tensor_scalar(rstd, newton2, c_(0, H_SCALE), None, ALU.mult).then_inc(stats_ready, 1)
            dve.wait_ge(stats_ready, 1)
            for j in range(DVE_NORMS):
                normalise(V, j).then_inc(x_normed, 1)

            scan_first(0)
            scan_first(1)
            dve.wait_ge(rows_made, 1)
            then(V.tensor_copy(row_f, pair[0:1, 0, 0:2 * GROUPS].rearrange("p (a g) -> p a g", a=2)))
            V.tensor_copy(row_i, row_f[:, 0, :])
            then(V.tensor_reduce(most_f, row_f[:, 1, :], AX.X, ALU.max))
            V.tensor_copy(most_i, most_f).then_inc(rows_kept, 1)

            for n in range(2, SCANS_BEFORE):
                scan_first(n)
            then(V.memset(hot_type[0:EMB_COLS], 0.0))
            for at in (0, LO_ROW):
                V.tensor_scalar(hot_type[at:at + TYPES], type_i[at:at + TYPES], part_id[at:at + TYPES], HOT,
                                ALU.is_equal, ALU.mult)
            for k in range(FULL_TILES[0]):
                dve.wait_ge(h0_hi, k + 1)
                for c, (c0, cw) in enumerate(H0_CHUNKS):
                    ins = V.scalar_tensor_tensor(out=h_a[:, 1, k, c0:c0 + cw], in0=trio[:, k % 2, c, 0:cw],
                                                 scalar=0.0, in1=h_a[:, 0, k, c0:c0 + cw],
                                                 op0=ALU.max, op1=ALU.subtract)
                ins.then_inc(h0_lo, 1)
                if k + SCANS_BEFORE < SCANS0:
                    scan_first(k + SCANS_BEFORE)

            def hot_rows(g, slot):
                dve.wait_ge(group_counted, g + RING_CREDIT - RING + 1)
                for u in range(SUBS - (slot in ACT_SLOTS)):
                    ins = V.tensor_scalar(ring_main[0:SUB, slot, u, :], iota_h[0:SUB, :],
                                          keys_t[:, 0, u, bass.ds(g, 1)], None, ALU.is_equal)
                ins.then_inc(main_hot, 1)

            def add_window(bank, first):
                view = counts[:, :, :, bass.ds(first, WIN)]
                return V.tensor_tensor(view, view, trio[:, 1, bank, 0:WIN_COLS].rearrange(
                    "p (j r d) -> p j r d", j=NODE_TILES, r=RELS), ALU.add)

            def first_of(g, groups=1):
                return nc.values_load_multi_w_load_instructions(
                    row_i[0:1, bass.ds(g, groups)], engines=(mybir.EngineType.DVE,), min_val=0, max_val=N - 1,
                    skip_runtime_bounds_check_because="minima of dst, whose values number the N nodes")[1]

            def add_group(g, bank, first):
                dve.wait_ge(group_counted, g + RING_CREDIT + 1)
                dve.wait_ge(group_added, g + BANK_CREDIT)
                add_window(bank, first).then_inc(group_added, 1)

            def scan(in_count, cols, at):
                dve.wait_ge(w_in, in_count)
                V.tensor_reduce(tile_max[:, bass.ds(at, 1)],
                                w_raw[:, 0:2 * cols], AX.X, ALU.max,
                                apply_absolute_value=True).then_inc(w_used, 1)

            def joined(n, column, maxima):
                V.tensor_reduce(local[:, column:column + 1], maxima, AX.X, ALU.max).then_inc(max_local, 1)
                dve.wait_ge(max_over_all, n)

            def weight_scales(l, n):
                if l:
                    dve.wait_ge(w_used, used_before(l - 1, T[l - 1] - 1) + 2)
                else:
                    dve.wait_ge(scans_done, 1)
                joined(n, 0, tile_max[:, 0:SCANS0 if l == 0 else 2 * K_TILES[l]])
                then(V.tensor_scalar(c_(l, W_MAX), over_all[:, 0:1], TINY, None, ALU.max))
                scale_of(l, W_MAX, W_SCALE, W_BACK, TOP_EMB if l == 0 else TOP).then_inc(scales_ready, 1)

            def message_scales(l):
                dve.wait_ge(scales_ready, w_scaled_at(l))
                then(V.tensor_tensor(c_(l, B1), c_(l, W_MAX), c_(l, W_SCALE), ALU.mult))
                then(V.tensor_tensor(c_(l, B1), c_(l, B1), c_(l, H_TOP), ALU.mult))
                then(V.tensor_scalar(c_(l, B1), c_(l, B1), K_BOUND, TINY, ALU.mult, ALU.max))
                then(scale_of(l, B1, M_SCALE, M_BACK))
                then(V.tensor_tensor(c_(l, ROOT_BACK), c_(l, H_BACK), c_(l, W_BACK), ALU.mult))
                ins = V.tensor_tensor(c_(l, REL_BACK), c_(l, ROOT_BACK), c_(l, M_BACK), ALU.mult)
                if l < LAST:
                    then(ins)
                    then(V.tensor_tensor(c_(l + 1, B2), c_(l, H_TOP), c_(l, H_BACK), ALU.mult))
                    then(V.tensor_tensor(c_(l + 1, B2), c_(l + 1, B2), c_(l, W_MAX), ALU.mult))
                    then(V.tensor_scalar(c_(l + 1, B2), c_(l + 1, B2), MATS * K_BOUND, bias_max[:],
                                         ALU.mult, ALU.add))
                    then(V.tensor_scalar(c_(l + 1, B2), c_(l + 1, B2), TINY, None, ALU.max))
                    ins = scale_of(l + 1, B2, H_SCALE, H_BACK)
                ins.then_inc(scales_ready, 1)
                dve.wait_ge(scales_ready, m_scaled_at(l))

            def low_w(l, half, nth_hi):
                ks, raw = own_view(l, half)
                dve.wait_ge(w_hi, nth_hi)
                to = w_split[:, 4 * half:4 * half + ks]
                V.scalar_tensor_tensor(out=to[:, :, 1].rearrange("p k m e -> p k (m e)"),
                                       in0=raw.rearrange("p (k e) -> p k e", k=ks), scalar=c_(l, W_SCALE),
                                       in1=to[:, :, 0].rearrange("p k m e -> p k (m e)"),
                                       op0=ALU.mult, op1=ALU.subtract).then_inc(w_used, 1)

            def low_embeddings(g):
                dve.wait_ge(emb_hi, g + 1)
                lo = emb_w[LO_ROW:EMB_ROWS]
                V.scalar_tensor_tensor(out=lo, in0=pair[LO_ROW:EMB_ROWS, 1, 0:MATS * P], scalar=1.0 / HOT,
                                       in1=lo, op0=ALU.mult, op1=ALU.subtract).then_inc(emb_split, 1)

            def low_message(l, g, j, bank, rows, msgs):
                dve.wait_ge(msg_hi, NODE_TILES * g + j + 1)
                hi, lo = (m[0:rows, bass.ds(j, 1), :].rearrange("p j e -> p (j e)") for m in msgs)
                V.scalar_tensor_tensor(out=lo, in0=pair[0:rows, bank, 0:RELS * P],
                                       scalar=c_(l, M_SCALE)[0:rows], in1=hi,
                                       op0=ALU.mult, op1=ALU.subtract).then_inc(msg_split, 1)

            def scan_next(l, t, half):
                scan(in_before(l, t) + (half + 1) * SCAN_INC, T[l + 1] * P, 2 * t + half)

            def count_rounds(it, rounds=1, between=None):
                firsts = first_of(it * RING, rounds * RING)
                for n in range(rounds):
                    for slot in range(RING):
                        g = (it + n) * RING + slot
                        add_group(g, slot % 2, firsts[n * RING + slot])
                        hot_rows(g + RING, slot)
                    if between is not None:
                        between(n)

            weight_scales(0, 2)
            message_scales(0)
            dve.wait_ge(counts_zeroed, 2)
            dve.wait_ge(rows_kept, 1)
            dve.wait_ge(keys_kept, 4)
            for slot in range(RING):
                hot_rows(slot, slot)
            count_rounds(0, ROUNDS_FIRST, lambda n: low_w(0, n, n + 1) if n < 2 else None)

            for b in range(EARLY):
                base = ROUNDS_FIRST + b * EARLY_ROUNDS
                low_embeddings(b)
                for half in range(2):
                    with dve.Fori(2 * half, 2 * half + 2) as jj:
                        count_rounds(base + 2 * jj, 2, lambda bank: low_message(
                            0, b, 2 * jj + bank, bank, P, early_msgs[b]))
                    scan_next(0, b, half)
                count_rounds(base + NODE_TILES - 2, 2, lambda n: low_message(
                    0, b, NODE_TILES - 2 + n, n, LAST_ROWS if n else P, early_msgs[b]))
                with dve.Fori(base + NODE_TILES, base + NODE_TILES + K_TILES[0] - 1, 2) as it:
                    count_rounds(it, 2)
                count_rounds(base + NODE_TILES + K_TILES[0] - 1)
                if b < EARLY - 1:
                    count_rounds(base + NODE_TILES + K_TILES[0], ROUNDS_SPLIT,
                                 lambda half: low_w(0, half, 2 * b + 2 + half + 1))
            firsts = first_of(GROUPS - RING, RING)
            for slot in range(RING):
                add_group(GROUPS - RING + slot, slot % 2, firsts[slot])

            most = dve.value_load(most_i, min_val=0, max_val=N // WIN)
            with dve.If(most > 0):
                dve.wait_ge(group_added, GROUPS + BANK_CREDIT)
                far_steps = Steps(dve, far_step)
                with dve.Fori(0, GROUPS) as g:
                    first = first_of(g)[0]
                    with dve.Fori(1, most + 1) as s:
                        v = dve.snap(g * most + s)
                        start = dve.snap((first + s * WIN) % (LAST_WIN + 1))
                        shift, rel, inside, key = far[:, 0:1], far[:, 1:3], far[:, 3:5], far[:, 5:7]
                        far_steps.base, far_steps.count = (v - 1) * FAR_STEPS, 0
                        fthen = far_steps.then
                        fthen(V.tensor_scalar(shift, iota_h[0:SUB, bass.ds(s, 1)], float(WIN), None, ALU.mult))
                        fthen(V.tensor_scalar(rel, keys_t[:, 3, :, bass.ds(g, 1)].rearrange("p u g -> p (u g)"),
                                              shift, None, ALU.subtract))
                        fthen(V.tensor_scalar(inside, rel, 0.0, None, ALU.is_ge))
                        fthen(V.tensor_tensor(key, keys_t[:, 2, :, bass.ds(g, 1)].rearrange("p u g -> p (u g)"),
                                              rel, ALU.add))
                        fthen(V.tensor_tensor(key, key, inside, ALU.mult))
                        fthen(V.scalar_tensor_tensor(out=key, in0=rel, scalar=float(WIN), in1=key,
                                                     op0=ALU.is_lt, op1=ALU.mult))
                        fthen(V.tensor_scalar(key, key, -1.0, None, ALU.add))
                        for u in range(SUBS):
                            V.tensor_scalar(ring_main[0:SUB, 0, u, :], iota_h[0:SUB, :], key[:, u:u + 1],
                                            None, ALU.is_equal)
                            ins = V.tensor_scalar(ring_src[0:SUB, 0, u, :], iota_h[0:SUB, 0:P],
                                                  keys_t[:, 1, u, bass.ds(g, 1)], None, ALU.is_equal)
                        ins.then_inc(far_hot, 1)
                        dve.wait_ge(far_counted, v)
                        add_window(0, start).then_inc(far_added, 1)
                        dve.wait_ge(far_added, v)

            dve.wait_ge(group_added, GROUPS + BANK_CREDIT)
            V.memset(local[:, 1:2], 0.0).then_inc(counts_done, 1)

            for r in range(RELS):
                dve.wait_ge(degrees_ready, r + 1)
                for c, (c0, cw) in enumerate(CHUNKS):
                    ins = V.tensor_scalar(inv[:, r, c0:c0 + cw], trio[:, r % 2, c, 0:cw], 1.0, None, ALU.max)
                ins.then_inc(degrees_taken, 1)
                if r == 0:
                    dve.wait_ge(degrees_taken, 1)
                    V.reciprocal(inv[:, 0, :], inv[:, 0, :]).then_inc(inverted, 1)
            dve.wait_ge(degrees_taken, RELS)
            V.reciprocal(inv[:, 1, :], inv[:, 1, :]).then_inc(inverted, 1)

            def add_relation(l, g, r, to, flip):
                dve.wait_ge(rel_ready, RELS * g + r + 1)
                for c, (c0, cw) in enumerate(CHUNKS):
                    nth = 9 * g + 3 * r + c
                    V.scalar_tensor_tensor(out=part[:, 0:cw], in0=trio[:, (r + 1 + flip) % 2, c, 0:cw],
                                           scalar=c_(l, REL_BACK), in1=inv[:, r, c0:c0 + cw],
                                           op0=ALU.mult, op1=ALU.mult).then_inc(rel_taken, 1)
                    dve.wait_ge(rel_taken, nth + 1 + SLOT_CREDIT)
                    if r == 0 and c == 0:
                        dve.wait_ge(root_taken, g + 1)
                    V.tensor_tensor(to[:, c0:c0 + cw], to[:, c0:c0 + cw], part[:, 0:cw],
                                    ALU.add).then_inc(rel_added, 1)
                    dve.wait_ge(rel_added, nth + 1)

            def add_residual(t):
                dve.wait_ge(out_turned, t + 1)
                dve.wait_ge(resid_in, 32 * (t + 1) + RESID_CREDIT)
                slot = dve.snap(t % 2)
                for bank, (j0, nj, rows) in enumerate(((0, 4, P), (4, 4, P), (8, 1, P), (9, 1, LAST_ROWS))):
                    view = resid[0:rows, bass.ds(slot, 1), j0:j0 + nj, :].rearrange("p s j c -> p (s j c)")
                    at = (j0 % 4) * P
                    ins = V.tensor_tensor(view, view, trio[0:rows, 0, j0 // 4, at:at + nj * P], ALU.add)
                ins.then_inc(out_added, 1)

            def add_block(l, t, to, next_l, nth_hi, flip=ROOT_SET, inverts=False):
                g = FIRST[l] + t
                for r in range(RELS):
                    if next_l is not None and r < 2:
                        low_w(next_l, r, nth_hi + r + 1)
                    if inverts:
                        dve.wait_ge(inverted, r + 1)
                    add_relation(l, g, r, to, flip)
                    if inverts and r == 0:
                        V.reciprocal(inv[:, 2, :], inv[:, 2, :]).then_inc(inverted, 1)
                if l == LAST:
                    return
                V.tensor_scalar(to[:], to[:], 0.0, c_(l + 1, H_SCALE), ALU.max,
                                ALU.mult).then_inc(h_scaled, 1)
                dve.wait_ge(h_scaled, g + 1)
                V.tensor_reduce(tile_max[:, bass.ds(2 * T[0] + t, 1)], to[:], AX.X, ALU.max)
                dve.wait_ge(h_hi, g + 1)
                h_next = h_in[l + 1]
                V.tensor_tensor(h_next[:, 1, bass.ds(t, 1), :].rearrange("p k n -> p (k n)"), to[:],
                                h_next[:, 0, bass.ds(t, 1), :].rearrange("p k n -> p (k n)"),
                                ALU.subtract).then_inc(block_done, 1)

            def last_relu():
                V.tensor_scalar(acc[:], acc[:], 0.0, None, ALU.max).then_inc(h_scaled, 1)

            def dve_block(l, t, next_l, adds):
                g = FIRST[l] + t
                if l == 0:
                    low_embeddings(g)
                for j in range(NODE_TILES):
                    low_message(l, g, j, j % 2, P if j < NODE_TILES - 1 else LAST_ROWS, msgs_a)
                    if l < LAST and j in (3, 7):
                        scan_next(l, t, j // 4)
                    if adds and j == 1:
                        last_relu()
                if l < LAST and next_l == l + 1:
                    weight_scales(l + 1, 3 + 2 * l)
                if adds:
                    add_residual(t - 1)
                add_block(l, t, acc, next_l, 2 * g + 2)

            for b in range(EARLY):
                add_block(0, b, early_accs[b], 0 if b == 1 else None, 2 * EARLY, b % 2, b == 0)
            for l in range(LAYERS):
                if l:
                    dve.wait_ge(block_done, FIRST[l] + DONE_CREDIT)
                    joined(2 + 2 * l, 1, tile_max[:, 2 * T[0]:2 * T[0] + T[l - 1]])
                    then(V.tensor_copy(c_(l, H_TOP), over_all[:, 1:2]))
                    message_scales(l)
                if l == LAST:
                    dve_block(l, 0, l, False)
                with dve.Fori(START[l], T[l] - 1) as t:
                    dve_block(l, t, l, l == LAST)
                dve_block(l, T[l] - 1, l + 1 if l < LAST else None, l == LAST)
            last_relu()
            add_residual(T[LAST] - 1)

        @block.tensor
        def _(pe):
            M = nc.tensor
            pe.sem_inc(group_counted, RING_CREDIT)
            pe.sem_inc(group_added, BANK_CREDIT)
            pe.sem_inc(msg_split, BANK_CREDIT)
            pe.sem_inc(rel_taken, SLOT_CREDIT)
            pe.sem_inc(stored, STORE_CREDIT)
            pe.sem_inc(resid_in, RESID_CREDIT)
            pe.sem_inc(block_done, DONE_CREDIT)
            pe.sem_inc(src_hot, SRC_CREDIT)
            pe.sem_inc(src_hot_b, SRC_B_CREDIT)

            pe.wait_ge(consts_made, 6)
            pe.wait_ge(small_in, 16 * (2 * TYPES + 1 + LAYERS))
            M.transpose(pair[:, 1, 0:BLOCKS], bias_rows, ident[0:BLOCKS, 0:BLOCKS])
            M.transpose(pair[:, 1, EMB_COLS:EMB_COLS + TYPES], emb, ident[0:TYPES, 0:TYPES]).then_inc(bias_turned, 1)
            pe.wait_ge(keys_made, 1)
            for a in range(4):
                for u in range(SUBS):
                    for h in range(HALVES):
                        at = u * GROUPS + h * GP
                        last = M.transpose(trio[0:SUB, a % 2, a // 2, at:at + GP], keys[:, a, h, u, :],
                                           ident[0:GP, 0:GP])
                last.then_inc(keys_turned, 1)
            for a, col in enumerate((lowest, extra)):
                for h in range(HALVES):
                    at = a * GROUPS + h * GP
                    last = M.matmul(pair[0:1, 0, at:at + GP], col[:, h:h + 1], ident[0:GP, 0:GP],
                                    start=True, stop=True, skip_group_check=True)
            last.then_inc(rows_made, 1)

            pe.wait_ge(keys_kept, 4)
            pe.wait_ge(x_normed, NODE_TILES)
            for k in range(FULL_TILES[0]):
                if k >= 2:
                    pe.wait_ge(h0_lo, k - 1)
                for j in range(NODE_TILES):
                    rows = P if j < NODE_TILES - 1 else LAST_ROWS
                    at = (j % 4) * P
                    last = M.transpose(trio[:, k % 2, j // 4, at:at + rows],
                                       x_sb[0:rows, j, k * P:(k + 1) * P], ident[0:rows, 0:rows])
                last.then_inc(h0_ready, 1)

            def count(slot, bank):
                for u in range(SUBS):
                    ins = M.matmul(trio[:, 1, bank, 0:WIN_COLS], ring_src[0:SUB, slot, u, :],
                                   ring_main[0:SUB, slot, u, :], start=(u == 0), stop=(u == SUBS - 1))
                return ins

            def count_round(it, beside=()):
                for slot in range(RING):
                    g = it * RING + slot
                    pe.wait_ge(main_hot, g + 1)
                    pe.wait_ge(src_hot, g + 1 + SRC_CREDIT)
                    pe.wait_ge(src_hot_b, g + 1 + SRC_B_CREDIT)
                    if slot in ACT_SLOTS:
                        pe.wait_ge(act_hot, len(ACT_SLOTS) * it + ACT_SLOTS.index(slot) + 1)
                    pe.wait_ge(group_added, g + BANK_CREDIT - 1)
                    count(slot, slot % 2).then_inc(group_counted, 1)
                    if slot < len(beside):
                        beside[slot]()

            def messages(l, g, j, bank, rows, w_count, shares=1):
                passes = [(k, ph, pw) for k in range(FULL_TILES[l]) for ph, pw in ((0, 0), (0, 1), (1, 0))]
                if l == 0:
                    passes.append(None)
                ends = [s * len(passes) // shares for s in range(shares + 1)]

                def share(s):
                    if s == 0:
                        pe.wait_ge(msg_split, NODE_TILES * g + j - 1 + BANK_CREDIT)
                        if w_count is not None:
                            pe.wait_ge(w_used, w_count)
                    for i in range(ends[s], ends[s + 1]):
                        if passes[i] is None:
                            pe.wait_ge(emb_split, g + 1)
                            stationary = hot_type[0:EMB_ROWS, bass.ds(j * P, rows)]
                            moving = emb_w[0:EMB_ROWS, 0:RELS * P]
                        else:
                            k, ph, pw = passes[i]
                            stationary = h_in[l][:, ph, k, bass.ds(j * P, rows)]
                            moving = w_split[:, k, pw, 0:RELS, :].rearrange("p m e -> p (m e)")
                        last = M.matmul(pair[0:rows, bank, 0:RELS * P], stationary, moving,
                                        start=(i == 0), stop=(i == len(passes) - 1))
                    if s == shares - 1:
                        last.then_inc(msg_ready, 1)
                return [lambda s=s: share(s) for s in range(shares)]

            def all_messages(l, g, w_count):
                messages(l, g, 0, 0, P, w_count)[0]()
                messages(l, g, 1, 1, P, None)[0]()
                with pe.Fori(1, NODE_TILES // 2 - 1) as jj:
                    for bank in range(2):
                        messages(l, g, 2 * jj + bank, bank, P, None)[0]()
                messages(l, g, NODE_TILES - 2, 0, P, None)[0]()
                messages(l, g, NODE_TILES - 1, 1, LAST_ROWS, None)[0]()

            def root_pass(l, k, n, first, final, to_set):
                pw, ph = ((0, 0), (0, 1), (1, 0))[n]
                for c, (c0, cw) in enumerate(CHUNKS):
                    last = M.matmul(trio[:, to_set, c, 0:cw],
                                    w_split[:, bass.ds(k, 1), pw, RELS, :].rearrange("p k e -> p (k e)"),
                                    h_in[l][:, ph, bass.ds(k, 1), c0:c0 + cw].rearrange("p k n -> p (k n)"),
                                    start=(first and n == 0), stop=(final and n == 2))
                return last

            def root_embeddings(g, to_set):
                pe.wait_ge(emb_split, g + 1)
                for c, (c0, cw) in enumerate(CHUNKS):
                    last = M.matmul(trio[:, to_set, c, 0:cw], emb_w[0:EMB_ROWS, RELS * P:MATS * P],
                                    hot_type[0:EMB_ROWS, c0:c0 + cw], start=False, stop=True)
                return last

            def root_tile(l, g, k):
                if k == FULL_TILES[l]:
                    return root_embeddings(g, ROOT_SET)
                for n in range(3):
                    last = root_pass(l, k, n, k == 0, k == K_TILES[l] - 1, ROOT_SET)
                return last

            def embeddings(g, w_count):
                pe.wait_ge(msg_split, NODE_TILES * g + BANK_CREDIT)
                pe.wait_ge(w_used, w_count)
                for n, (part_e, pw) in enumerate(((0, 0), (0, 1), (1, 0))):
                    last = M.matmul(pair[0:EMB_COLS, 1, 0:MATS * P], emb_t[:, part_e, :],
                                    w_split[:, FULL_TILES[0], pw].rearrange("p m e -> p (m e)"),
                                    start=(n == 0), stop=(n == 2))
                last.then_inc(emb_ready, 1)

            def gather_tile(msgs, r, slot, j, rows, start, stop):
                for pm in range(2):
                    for c, (c0, cw) in enumerate(CHUNKS):
                        last = M.matmul(trio[:, slot, c, 0:cw],
                                        msgs[pm][0:rows, bass.ds(j, 1), r * P:(r + 1) * P].rearrange("p j e -> p (j e)"),
                                        counts[0:rows, bass.ds(j, 1), r, c0:c0 + cw].rearrange("p j n -> p (j n)"),
                                        start=start and pm == 0, stop=stop and pm == 1)
                return last

            def gathering(g, msgs, flip=ROOT_SET):
                pe.wait_ge(msg_split, NODE_TILES * (g + 1) - 1 + BANK_CREDIT)
                for r in range(RELS):
                    if isinstance(g, int) and g == 0:
                        if r < 2:
                            pe.wait_ge(degrees_taken, r + 2)
                        else:
                            pe.wait_ge(rel_taken, 3 + SLOT_CREDIT)
                    elif isinstance(g, int) and g < EARLY:
                        pe.wait_ge(rel_taken, 9 * g + 3 * (r - 1) + SLOT_CREDIT)
                    elif r == 1:
                        pe.wait_ge(root_taken, g + 1)
                    else:
                        pe.wait_ge(rel_taken, 9 * g + (3 if r == 2 else 0) + SLOT_CREDIT)
                    slot = (r + 1 + flip) % 2
                    gather_tile(msgs, r, slot, 0, P, True, False)
                    with pe.Fori(1, NODE_TILES - 1, 2) as j:
                        gather_tile(msgs, r, slot, j, P, False, False)
                        gather_tile(msgs, r, slot, j + 1, P, False, False)
                    if r == 0:
                        pe.wait_ge(msg_split, NODE_TILES * (g + 1) + BANK_CREDIT)
                    gather_tile(msgs, r, slot, NODE_TILES - 1, LAST_ROWS, False, True).then_inc(rel_ready, 1)

            def turn_out(t):
                pe.wait_ge(h_scaled, FIRST[LAST] + t + 1)
                pe.wait_ge(rel_taken, 9 * (FIRST[LAST] + t + 1) + SLOT_CREDIT)
                for j in range(NODE_TILES):
                    rows = P if j < NODE_TILES - 1 else LAST_ROWS
                    at = (j % 4) * P
                    last = M.transpose(trio[0:rows, 0, j // 4, at:at + P], acc[:, j * P:j * P + rows], ident[:])
                last.then_inc(out_turned, 1)

            def pe_block(l, t):
                g = FIRST[l] + t
                all_messages(l, g, used_before(l, t))
                turn_out(t - 1)
                pe.wait_ge(rel_taken, 9 * g - 3 + SLOT_CREDIT)
                for k in range(K_TILES[l]):
                    last = root_tile(l, g, k)
                last.then_inc(root_ready, 1)
                pe.wait_ge(out_added, t)
                gathering(g, msgs_a)

            def root_first_block(l, t, first):
                g = FIRST[l] + t
                final = K_TILES[l] - 1
                pe.wait_ge(rel_taken, 9 * g - 3 + SLOT_CREDIT)
                pe.wait_ge(w_used, used_before(l, t))
                if l == 0:
                    embeddings(g, used_before(l, t))
                if first:
                    pe.wait_ge(block_done, g - 1 + DONE_CREDIT)
                for k in range(final):
                    root_tile(l, g, k)
                if first:
                    pe.wait_ge(block_done, g + DONE_CREDIT)
                root_tile(l, g, final).then_inc(root_ready, 1)
                all_messages(l, g, None)
                gathering(g, msgs_a)

            pe.wait_ge(rows_kept, 1)
            pe.wait_ge(h0_lo, FULL_TILES[0])
            with pe.Fori(0, ROUNDS_FIRST) as it:
                count_round(it)
            for b in range(EARLY):
                base = ROUNDS_FIRST + b * EARLY_ROUNDS
                w_count = used_before(0, b)
                embeddings(b, w_count)
                with pe.Fori(0, NODE_TILES // 2 - 1) as jj:
                    for bank in range(2):
                        count_round(base + 2 * jj + bank,
                                    messages(0, b, 2 * jj + bank, bank, P, w_count, RING - 1))
                for j in range(NODE_TILES - 2, NODE_TILES):
                    count_round(base + j, messages(0, b, j, j % 2, P if j < NODE_TILES - 1 else LAST_ROWS,
                                                   w_count, RING - 1))
                if b:
                    pe.wait_ge(root_taken, b)
                base += NODE_TILES
                def root_passes(k, first, final):
                    return [lambda n=n: root_pass(0, k, n, first, final, 0) for n in range(RING - 1)]

                count_round(base, root_passes(0, True, False))
                with pe.Fori(1, K_TILES[0] - 1) as k:
                    count_round(base + k, root_passes(k, False, False))
                count_round(base + K_TILES[0] - 1, [lambda: root_embeddings(b, 0).then_inc(root_ready, 1)])
                base += K_TILES[0]
                with pe.Fori(base, base + ROUNDS_SPLIT if b < EARLY - 1 else ROUNDS) as it:
                    count_round(it)
            most = pe.value_load(most_i, min_val=0, max_val=N // WIN)
            with pe.If(most > 0):
                with pe.Fori(0, GROUPS * most) as v:
                    pe.wait_ge(far_hot, v + 1)
                    count(0, 0).then_inc(far_counted, 1)

            pe.wait_ge(counts_done, 1)
            pe.wait_ge(root_taken, EARLY)
            for r in range(RELS):
                if r == 2:
                    pe.wait_ge(degrees_taken, 1)
                for j in range(NODE_TILES):
                    for c, (c0, cw) in enumerate(CHUNKS):
                        last = M.matmul(trio[:, r % 2, c, 0:cw], ones_h[:], counts[:, j, r, c0:c0 + cw],
                                        start=(j == 0), stop=(j == NODE_TILES - 1))
                last.then_inc(degrees_ready, 1)
            for b in range(EARLY):
                gathering(b, early_msgs[b], b % 2)
            for l in range(LAYERS):
                if l:
                    root_first_block(l, 0, True)
                with pe.Fori(1 if l else EARLY, T[l]) as t:
                    if l == LAST:
                        pe_block(l, t)
                    else:
                        root_first_block(l, t, False)
            turn_out(T[LAST] - 1)


_INS = ['x', 'src', 'dst', 'edge_type_3', 'node_type_3', 'L0_gnn_node_emb', 'L0_gnn_w_rel1', 'L0_gnn_w_root1',
        'L0_gnn_b1', 'L0_gnn_w_rel2', 'L0_gnn_w_root2', 'L0_gnn_b2', 'L0_gnn_w_rel3', 'L0_gnn_w_root3', 'L0_gnn_b3']
_OUTS = [((N, 768), 'float32')]


def kernel(**inputs):
    import numpy as _np
    import concourse.bacc as _bacc
    from concourse import mybir as _mybir
    from concourse.bass_utils import run_bass_kernel_spmd as _run

    nc = _bacc.Bacc("TRN2", target_bir_lowering=False, num_devices=1)
    arrays, args = {}, []
    for name in _INS:
        a = _np.ascontiguousarray(inputs[name])
        arrays[f"in_{name}_dram"] = a
        args.append(nc.dram_tensor(f"in_{name}_dram", a.shape, _mybir.dt.from_np(a.dtype), kind="ExternalInput").ap())
    for i, (shape, dtype) in enumerate(_OUTS):
        dt = _mybir.dt.from_np(_np.dtype(dtype))
        args.append(nc.dram_tensor(f"out_{i}_dram", shape, dt, kind="ExternalOutput").ap())
    gnn_kernel(nc, *args)
    r = _run(nc, [arrays], core_ids=[0])
    got = tuple(r.results[0][f"out_{i}_dram"] for i in range(len(_OUTS)))
    return got[0]
```
